# Optimizing a Trainium2 kernel written in Bass

```python
import numpy as np
import jax
import jax.numpy as jnp

def _softmax(x, axis=-1):
    return jax.nn.softmax(x, axis=axis)

def _gelu(x):
    return jax.nn.gelu(x, approximate=True)

def _silu(x):
    return jax.nn.silu(x)

def _sigmoid(x):
    return jax.nn.sigmoid(x)

def _layernorm(x, axis=-1, eps=1e-05):
    m = jnp.mean(x, axis=axis, keepdims=True)
    v = jnp.var(x, axis=axis, keepdims=True)
    return (x - m) / jnp.sqrt(v + eps)

def _scatter_add(tgt, idx, src, axis=0):
    return tgt.at[idx].add(src)

def _segment_sum(src, seg, n):
    return jax.ops.segment_sum(src, seg, n)
kernel_name = 'mk_cond_resid_d2_seqx_r4_f5b6bb'

def setup_inputs(seed: int=0):
    np.random.seed(seed)
    _w = jnp.asarray

    def _rec_inputs():
        import jax
        import jax.numpy as jnp
        _rk = jax.random.key(seed)
        x = -0.000125 + 0.9999 * jax.random.normal(jax.random.fold_in(_rk, 1), (16, 256, 256), jnp.float32)
        _lenS = 256 - jax.random.randint(jax.random.fold_in(_rk, 7), (16,), 0, max(1, 256 // 4) + 1, jnp.int32)
        _lenS2 = 256 - jax.random.randint(jax.random.fold_in(_rk, 8), (16,), 0, max(1, 256 // 4) + 1, jnp.int32)
        cond_1024 = -0.00493535 + 1.00056 * jax.random.normal(jax.random.fold_in(_rk, 11), (16, 256), jnp.float32)
        return (x, cond_1024)
    x, cond_1024 = _rec_inputs()

    def _L0_cond_setup():
        import jax, jax.numpy as jnp
        import numpy as np
        import math
        D = 256
        H = 256
        key = jax.random.key(seed)
        k1, k2, k3, k4 = jax.random.split(key, 4)
        x = jax.random.normal(k1, (64, 128, D), dtype=jnp.float32)
        h0 = jax.random.normal(k2, (64, H), dtype=jnp.float32)
        Wx = jax.random.normal(k3, (D, 4 * H), dtype=jnp.float32) / math.sqrt(D)
        Wh = jax.random.normal(k4, (H, 4 * H), dtype=jnp.float32) / math.sqrt(H)
        b = jnp.zeros((4 * H,), dtype=jnp.float32)
        return {'x': x, 'h0': h0, 'Wx': Wx, 'Wh': Wh, 'b': b}
    _L0_cond_all = _L0_cond_setup()
    _L0_cond_in = {k: v for k, v in _L0_cond_all.items() if k in ('Wx', 'Wh', 'b')}
    del _L0_cond_all

    def _L1_cond_setup():
        import jax, jax.numpy as jnp
        import numpy as np
        RANK = 8
        LN_EPS = 1e-05
        key = jax.random.key(seed)
        ks = jax.random.split(key, 8)
        B, T, D = (16, 256, 256)
        A = 256
        I = 256
        OUT = D * RANK * 4
        s = 0.02
        return {'x': jax.random.normal(ks[0], (B, T, D), jnp.float32), 'ada_emb': jax.random.normal(ks[1], (B, A), jnp.float32), 'base_up': jax.random.normal(ks[2], (D, D), jnp.float32) * s, 'base_down': jax.random.normal(ks[3], (D, D), jnp.float32) * s, 'ln_gamma': jnp.ones((A,), jnp.float32), 'ln_beta': jnp.zeros((A,), jnp.float32), 'W1': jax.random.normal(ks[4], (A, I), jnp.float32) / np.sqrt(A), 'bias1': jnp.zeros((I,), jnp.float32), 'W2': jax.random.normal(ks[5], (I, OUT), jnp.float32) / np.sqrt(I), 'bias2': jnp.zeros((OUT,), jnp.float32)}
    _L1_cond_all = _L1_cond_setup()
    _L1_cond_in = {k: v for k, v in _L1_cond_all.items() if k in ('base_up', 'base_down', 'ln_gamma', 'ln_beta', 'W1', 'bias1', 'W2', 'bias2')}
    del _L1_cond_all
    return {'x': x, 'cond_1024': cond_1024, 'L0_cond_Wx': _L0_cond_in['Wx'], 'L0_cond_Wh': _L0_cond_in['Wh'], 'L0_cond_b': _L0_cond_in['b'], 'L1_cond_base_up': _L1_cond_in['base_up'], 'L1_cond_base_down': _L1_cond_in['base_down'], 'L1_cond_ln_gamma': _L1_cond_in['ln_gamma'], 'L1_cond_ln_beta': _L1_cond_in['ln_beta'], 'L1_cond_W1': _L1_cond_in['W1'], 'L1_cond_bias1': _L1_cond_in['bias1'], 'L1_cond_W2': _L1_cond_in['W2'], 'L1_cond_bias2': _L1_cond_in['bias2']}

def reference(x, cond_1024, L0_cond_Wx, L0_cond_Wh, L0_cond_b, L1_cond_base_up, L1_cond_base_down, L1_cond_ln_gamma, L1_cond_ln_beta, L1_cond_W1, L1_cond_bias1, L1_cond_W2, L1_cond_bias2):
    import jax
    import jax.numpy as jnp

    def _L0_cond_ref(x, h0, Wx, Wh, b):
        import jax, jax.numpy as jnp
        import numpy as np
        import math
        D = 256
        H = 256
        xz = jnp.einsum('ntd,dk->ntk', x, Wx) + b
        c0 = jnp.zeros_like(h0)

        def step(carry, xz_t):
            prev_h, prev_c = carry
            z = xz_t + prev_h @ Wh
            ai, af, ao, ag = jnp.split(z, 4, axis=1)
            i = jax.nn.sigmoid(ai)
            f = jax.nn.sigmoid(af)
            o = jax.nn.sigmoid(ao)
            g = jnp.tanh(ag)
            next_c = f * prev_c + i * g
            next_h = o * jnp.tanh(next_c)
            return ((next_h, next_c), next_h)
        _, hs = jax.lax.scan(step, (h0, c0), jnp.swapaxes(xz, 0, 1))
        return jnp.swapaxes(hs, 0, 1)

    def _L1_cond_ref(x, ada_emb, base_up, base_down, ln_gamma, ln_beta, W1, bias1, W2, bias2):
        import jax, jax.numpy as jnp
        import numpy as np
        RANK = 8
        LN_EPS = 1e-05
        B, T, D = x.shape
        R = RANK
        mu = jnp.mean(ada_emb, axis=-1, keepdims=True)
        var = jnp.mean(jnp.square(ada_emb - mu), axis=-1, keepdims=True)
        c = (ada_emb - mu) / jnp.sqrt(var + LN_EPS) * ln_gamma + ln_beta
        h = jax.nn.gelu(c @ W1 + bias1, approximate=False)
        w = h @ W2 + bias2
        a1, b1, a2, b2 = [t.reshape(B, D, R) for t in jnp.split(w, 4, axis=-1)]
        u = jnp.einsum('btd,bdr->btr', x, a2)
        mid = jnp.einsum('btd,dl->btl', x, base_down) + jnp.einsum('btr,blr->btl', u, b2)
        mid = jax.nn.gelu(mid, approximate=False)
        v = jnp.einsum('blr,btl->btr', b1, mid)
        out = jnp.einsum('btl,kl->btk', mid, base_up) + jnp.einsum('bkr,btr->btk', a1, v)
        return x + out
    x = x + _L0_cond_ref(x, cond_1024, L0_cond_Wx, L0_cond_Wh, L0_cond_b)
    x = x + _L1_cond_ref(x, cond_1024, L1_cond_base_up, L1_cond_base_down, L1_cond_ln_gamma, L1_cond_ln_beta, L1_cond_W1, L1_cond_bias1, L1_cond_W2, L1_cond_bias2)
    return x

_drawn_inputs = setup_inputs


def setup_inputs(seed=0):
    import zlib

    import numpy as np

    out = dict(_drawn_inputs(seed))
    spreads = {'L0_cond_b': (0.0, 0.1),
     'L1_cond_ln_gamma': (1.0, 0.2),
     'L1_cond_ln_beta': (0.0, 0.1),
     'L1_cond_bias1': (0.0, 0.1),
     'L1_cond_bias2': (0.0, 0.1)}
    factors = {'L1_cond_base_up': 4.036, 'L1_cond_base_down': 3.93}
    for name, (base, spread) in spreads.items():
        noise = np.random.default_rng([zlib.crc32(name.encode()), seed]).standard_normal(out[name].shape)
        drawn = base * np.exp(spread * noise) if base else spread * noise
        out[name] = jnp.asarray(drawn.astype(out[name].dtype))
    for name, factor in factors.items():
        out[name] = (out[name] * factor).astype(out[name].dtype)
    return out
```

```python
from contextlib import ExitStack

import concourse.bass as bass
from concourse import mybir

F32 = mybir.dt.float32
ALU = mybir.AluOpType
ACT = mybir.ActivationFunctionType
AX = mybir.AxisListType

B, T, D, H = 16, 256, 256, 256
G = 4
P = 128
NQ, NM, C = 4, 2, 32
TB = 8
NBLK = T // TB
RANK = 8
GC = G * C
ZW = NM * GC
XQ = 4
XW = G * H // XQ
LN_EPS = 1e-5
LAG = 1


def lstm_adapter(nc, x, cond, Wx, Wh, b, base_up, base_down, gamma, beta, W1, bias1, W2, bias2, out):
    ctx = ExitStack()
    with ctx:
        def sb(name, shape):
            return ctx.enter_context(nc.sbuf_tensor(name, shape, F32))

        def psum(name):
            return ctx.enter_context(nc.psum_tensor(name, [P, 512], F32))

        def sem(name):
            return ctx.enter_context(nc.semaphore(name))

        ident = sb("ident", [P, P])
        zeros = sb("zeros", [P, P])
        one_win = sb("one_win", [1, 3 * B])
        own_row = sb("own_row", [P, B])
        neg_half = sb("neg_half", [B, 1])
        wx_raw = sb("wx_raw", [P, NM, G * H])
        wh_raw = sb("wh_raw", [P, NM, G * H])
        b_raw = sb("b_raw", [P, G * H])
        wx = sb("wx", [P, NM, G * H])
        wh = sb("wh", [P, NM, G * H])
        b_all = sb("b_all", [P, G * H])
        down_raw = sb("down_raw", [P, NM, D])
        down = sb("down", [P, NM, D])
        up_raw = sb("up_raw", [P, NM, D])
        up_t = sb("up_t", [P, 2, D])
        a1_t = sb("a1_t", [P, D])
        b2_t = sb("b2_t", [P, D])
        b1_w = sb("b1_w", [P, 2, P])
        a2_w = sb("a2_w", [P, NM, P])
        c_in = sb("c_in", [B, D])
        c_gamma = sb("c_gamma", [B, D])
        c_beta = sb("c_beta", [B, D])
        c_mid = sb("c_mid", [B, D])
        c_sq = sb("c_sq", [B, D])
        c_norm = sb("c_norm", [B, D])
        c_stat = sb("c_stat", [B, 5])
        c_t = sb("c_t", [P, 2, B])
        w1 = sb("w1", [P, 2, D])
        b1_col = sb("b1_col", [P, 2])
        hid_win = sb("hid_win", [P, 2, 3 * B])
        w2 = [sb(f"w2_{i}", [P, 2, D * RANK]) for i in range(2)]
        b2_row = sb("b2_row", [1, 4, D * RANK])
        w_tmp = sb("w_tmp", [P, 2, D])
        x_nat = [sb(f"x_nat{i}", [P, D]) for i in range(2)]
        x_perm = [sb(f"x_perm{i}", [P, D]) for i in range(2)]
        x_t = [sb(f"x_t{i}", [P, NM, P]) for i in range(2)]
        x_keep = [sb(f"x_keep{i}", [P, NM, P]) for i in range(2)]
        proj = sb("proj", [P, G * H])
        seed = [sb(f"seed{i}", [P, TB, ZW]) for i in range(2)]
        cond_q = sb("cond_q", [P, NM * C])
        cond_2 = sb("cond_2", [P, NM * C])
        h_first = sb("h_first", [P, NM, 32])
        gates = [[sb(f"gates{i}_{m}", [P, GC + C]) for m in range(NM)] for i in range(2)]
        prod = [sb(f"prod{m}", [P, 2 * C]) for m in range(NM)]
        tanc = [sb(f"tanc{m}", [P, C]) for m in range(NM)]
        hid = [sb(f"hid{m}", [P, C]) for m in range(NM)]
        h_t = [sb(f"h_t{i}", [P, NM, TB, 32]) for i in range(2)]
        xp = [sb(f"xp{i}", [P, NM, P]) for i in range(2)]
        u_own = sb("u_own", [P, P])
        v_own = sb("v_own", [P, P])
        act_t = sb("act_t", [P, 2, P])
        y_t = sb("y_t", [P, NM, P])
        y_nat = [sb(f"y_nat{i}", [P, D]) for i in range(2)]

        z_bank = [[psum(f"z{i}_{m}") for m in range(NM)] for i in range(2)]
        aux = psum("aux")
        out_bank = psum("out_bank")
        x_bank = [psum(f"x_bank{i}") for i in range(2)]

        consts_made = sem("consts_made")
        zeroed = sem("zeroed")
        w_loaded = {n: sem(f"{n}_loaded") for n in
                    ("wx", "wh", "b", "down", "up", "cond", "cq", "w1", "b2row")}
        w2_loaded = [sem(f"w2_loaded{i}") for i in range(2)]
        wx_ready, wh_ready = sem("wx_ready"), sem("wh_ready")
        b_ready, down_ready = sem("b_ready"), sem("down_ready")
        bits_set = sem("bits_set")
        cond_doubled = sem("cond_doubled")
        ln_step, ln_pow = sem("ln_step"), sem("ln_pow")
        hyp_psum, hyp_copied = sem("hyp_psum"), sem("hyp_copied")
        x_loaded = [sem(f"x_loaded{i}") for i in range(2)]
        x_permuted = sem("x_permuted")
        xt_psum, xt_ready = sem("xt_psum"), sem("xt_ready")
        x_kept = sem("x_kept")
        xz_psum, xz_ready = sem("xz_psum"), sem("xz_ready")
        seed_loaded = [sem(f"seed_loaded{i}") for i in range(2)]
        both = range(NM)
        seeded = [sem(f"seeded{m}") for m in both]
        z_ready = [sem(f"z_ready{m}") for m in both]
        gates_ready = [sem(f"gates_ready{m}") for m in both]
        prod_ready = [sem(f"prod_ready{m}") for m in both]
        cell_ready = [sem(f"cell_ready{m}") for m in both]
        tanc_ready = [sem(f"tanc_ready{m}") for m in both]
        hid_ready = [sem(f"hid_ready{m}") for m in both]
        ht_ready = [sem(f"ht_ready{m}") for m in both]
        xp_ready = sem("xp_ready")
        u_psum, u_ready = sem("u_psum"), sem("u_ready")
        mid_psum, act_ready = sem("mid_psum"), sem("act_ready")
        v_psum, v_ready = sem("v_psum"), sem("v_ready")
        out_psum, y_ready = sem("out_psum"), sem("y_ready")
        yt_psum, y_copied = sem("yt_psum"), sem("y_copied")
        stored = [sem(f"stored{i}") for i in range(2)]

        block = ctx.enter_context(nc.Block())

        def perm(ap):
            return ap.rearrange("p (j m c) -> p m j c", j=NQ, m=NM)

        class Blk:

            def __init__(self, it, par, shift=0):
                self.k = it * 2 + (par + shift)
                self.par = (par + shift) % 2
                self.turn = it + (par + shift) // 2
                self.it, self.p, self.s = it, par, shift

            def plus(self, n):
                return Blk(self.it, self.p, self.s + n)

            def at_least(self, n):
                return not isinstance(self.k, int) or self.k >= n

            def exists(self):
                return not isinstance(self.k, int) or 0 <= self.k < NBLK

        def schedule(eng, one_block, last=1):
            for par in range(2):
                one_block(Blk(0, par), par >= LAG, True)
            with eng.Fori(1, NBLK // 2 - last) as it:
                for par in range(2):
                    one_block(Blk(it, par), True, True)
            for pair in range(NBLK // 2 - last, NBLK // 2):
                for par in range(2):
                    one_block(Blk(pair, par), True, pair < NBLK // 2 - 1)

        tail = [Blk(NBLK // 2, i) for i in range(LAG + 1)]

        @block.sync
        def _(sp):
            def load_x(f):
                first = f.k * TB if isinstance(f.k, int) else sp.snap(f.k * TB)
                if f.at_least(2):
                    sp.wait_ge(x_permuted, f.k - 1)
                sp.dma_start(x_nat[f.par][:, :], x[:, bass.ds(first, TB), :]).then_inc(x_loaded[f.par], 16)

            def load_seed(f):
                consumed = f.k * TB - TB if isinstance(f.k, int) else sp.snap(f.k * TB - TB)
                if f.at_least(2):
                    for m in both:
                        sp.wait_ge(seeded[m], consumed)
                sp.wait_ge(xz_ready, f.k * XQ + XQ)
                for j in range(NQ):
                    sp.dma_start(seed[f.par][32 * j:32 * j + B, :, :], proj[:, ZW * j:ZW * (j + 1)])\
                      .then_inc(seed_loaded[f.par], 16)

            def store_y(a):
                first = a.k * TB if isinstance(a.k, int) else sp.snap(a.k * TB)
                sp.wait_ge(y_copied, a.k + 1)
                sp.dma_start(out[:, bass.ds(first, TB), :], y_nat[a.par][:, :]).then_inc(stored[a.par], 16)

            by_half = "(j m c) n -> m j c n"
            load_x(Blk(0, 0))
            for m in both:
                sp.dma_start(wx_raw[:, m, :], Wx.rearrange(by_half, j=NQ, m=NM)[m]).then_inc(w_loaded["wx"], 16)
            load_x(Blk(0, 1))
            sp.dma_start(b_raw[:, :], b.partition_broadcast(P)).then_inc(w_loaded["b"], 16)
            for m in both:
                sp.dma_start(wh_raw[:, m, :], Wh.rearrange(by_half, j=NQ, m=NM)[m]).then_inc(w_loaded["wh"], 16)
            for m in both:
                sp.dma_start(up_raw[:, m, :], base_up.rearrange(by_half, j=NQ, m=NM)[m]).then_inc(w_loaded["up"], 16)
            for m in both:
                sp.dma_start(down_raw[:, m, :], base_down.rearrange(by_half, j=NQ, m=NM)[m])\
                  .then_inc(w_loaded["down"], 16)
            load_seed(Blk(0, 0))
            load_x(Blk(0, 0, 2))
            load_seed(Blk(0, 1))

            def one_block(k, adapter, front):
                if k.plus(3).exists():
                    load_x(k.plus(3))
                if k.plus(-LAG - 1).exists():
                    store_y(k.plus(-LAG - 1))
                if front:
                    load_seed(k.plus(2))

            schedule(sp, one_block, 2)
            for a in tail:
                store_y(a.plus(-LAG - 1))
            for i in range(2):
                sp.wait_ge(stored[i], 16 * (NBLK // 2))

        @block.scalar
        def _(act):
            act.dma_start(c_in[:, :], cond).then_inc(w_loaded["cond"], 16)
            act.wait_ge(zeroed, 2)
            for j in range(NQ):
                act.dma_start(cond_q[32 * j:32 * j + B, :], cond[:, NM * C * j:NM * C * (j + 1)])\
                   .then_inc(w_loaded["cq"], 16)
            act.dma_start(c_gamma[:, :], gamma.partition_broadcast(B)).then_inc(w_loaded["cond"], 16)
            act.dma_start(c_beta[:, :], beta.partition_broadcast(B)).then_inc(w_loaded["cond"], 16)
            act.dma_start(w1[:, :, :], W1.rearrange("(k p) n -> p k n", p=P)).then_inc(w_loaded["w1"], 16)
            act.dma_start(b1_col[:, :], bias1.rearrange("(k p) -> p k", p=P),
                          allow_slow_non_contiguous=True).then_inc(w_loaded["w1"], 16)
            w2_q = W2.rearrange("(k p) (q n) -> q p k n", p=P, q=4)
            for q in range(2):
                act.dma_start(w2[q][:, :, :], w2_q[q]).then_inc(w2_loaded[q], 16)

            def evacuate_x(f):
                act.wait_ge(xt_psum, f.k + 1)
                if f.at_least(2):
                    act.wait_ge(xz_psum, (f.k - 1) * XQ)
                    act.wait_ge(x_kept, f.k - 1)
                act.activation(x_t[f.par][:, :, :], aux[:, 0:NM * P].rearrange("p (m t) -> p m t", m=NM),
                               ACT.Copy, scale=0.5).then_inc(xt_ready, 1)

            def seed_bank(buf, s, m):
                act.activation(z_bank[s % 2][m][:, 0:GC], seed[buf][:, s, GC * m:GC * (m + 1)], ACT.Copy)\
                   .then_inc(seeded[m], 1)

            def gelu_mid(a):
                act.wait_ge(mid_psum, a.k + 1)
                if a.at_least(1):
                    act.wait_ge(out_psum, a.k)
                act.activation(act_t[:, :, :], aux[:, 0:2 * P].rearrange("p (l t) -> p l t", l=2),
                               ACT.Gelu).then_inc(act_ready, 1)

            def copy_y(a):
                act.wait_ge(yt_psum, a.k + 1)
                if a.at_least(2):
                    act.wait_ge(stored[a.par], a.turn * 16)
                act.activation(perm(y_nat[a.par][:, :]),
                               out_bank[:, 0:D].rearrange("p (m j c) -> p m j c", m=NM, j=NQ),
                               ACT.Copy).then_inc(y_copied, 1)

            act.wait_ge(w_loaded["w1"], 32)
            act.wait_ge(hyp_psum, 2)
            act.wait_ge(zeroed, 3)
            for i in range(2):
                act.activation(hid_win[:, i, B:2 * B], out_bank[:, i * B:(i + 1) * B], ACT.Gelu,
                               bias=b1_col[:, i:i + 1]).then_inc(hyp_copied, 1)
            for q in range(4):
                act.wait_ge(hyp_psum, 3 + q)
                src = x_bank[q % 2][:, 0:D]
                if q == 0:
                    ins = act.activation(a1_t[:, :].rearrange("p (m j c) -> p m j c", m=NM, j=NQ), perm(src), ACT.Copy)
                elif q == 1:
                    ins = act.activation(w_tmp[:, 0, :], src, ACT.Copy)
                elif q == 2:
                    ins = act.activation(w_tmp[:, 1, :].rearrange("p (m j c) -> p m j c", m=NM, j=NQ), perm(src),
                                         ACT.Copy, scale=0.5)
                else:
                    ins = act.activation(b2_t[:, :], src, ACT.Copy)
                ins.then_inc(hyp_copied, 1)
                if q < 2:
                    act.dma_start(w2[q][:, :, :], w2_q[q + 2]).then_inc(w2_loaded[q], 16)
            for n, dst in enumerate((b1_w, a2_w)):
                act.wait_ge(hyp_psum, 7 + n)
                act.activation(dst[:, :, :], x_bank[n][:, 0:2 * P].rearrange("p (l t) -> p l t", l=2), ACT.Copy)\
                   .then_inc(hyp_copied, 1)
            for i in range(2):
                act.wait_ge(hyp_psum, 9 + i)
                act.activation(up_t[:, i, :], (out_bank, aux)[i][:, 0:D], ACT.Copy).then_inc(hyp_copied, 1)

            for par in range(2):
                evacuate_x(Blk(0, par))
            act.wait_ge(bits_set, 1)
            act.wait_ge(seed_loaded[0], 16 * NQ)
            for s in range(2):
                for m in both:
                    seed_bank(0, s, m)

            def one_block(k, adapter, front):
                for s in range(TB):
                    n = k.k * TB + (s + 1)
                    for m in both:
                        act.wait_ge(z_ready[m], n)
                        act.activation(gates[s % 2][m][:, 0:GC], z_bank[s % 2][m][:, 0:GC], ACT.Tanh,
                                       scale=0.5).then_inc(gates_ready[m], 1)
                    for m in both:
                        act.wait_ge(cell_ready[m], n)
                        act.activation(tanc[m][:, :], gates[(s + 1) % 2][m][:, GC:GC + C], ACT.Tanh,
                                       scale=0.5).then_inc(tanc_ready[m], 1)
                    if s < TB - 2 or front or k.p == 0:
                        ahead = k if s < TB - 2 else k.plus(1)
                        if s == TB - 2:
                            act.wait_ge(seed_loaded[ahead.par], (ahead.turn + 1) * (16 * NQ))
                        for m in both:
                            seed_bank(ahead.par, (s + 2) % TB, m)
                    if s == 0 and front:
                        evacuate_x(k.plus(2))
                    if s == 1 and k.plus(-LAG - 1).exists():
                        copy_y(k.plus(-LAG - 1))
                    if s == 4 and adapter:
                        gelu_mid(k.plus(-LAG))

            schedule(act, one_block)
            for a in tail:
                copy_y(a.plus(-LAG - 1))
                if a is not tail[-1]:
                    gelu_mid(a.plus(-LAG))

        @block.tensor
        def _(pe):
            def transpose_x(f):
                pe.wait_ge(x_permuted, f.k + 1)
                for m in both:
                    ins = pe.transpose(aux[:, m * P:(m + 1) * P], x_perm[f.par][:, m * P:(m + 1) * P], ident[:, :])
                ins.then_inc(xt_psum, 1)

            def project(f, q, kc):
                if q == 0 and kc == 0:
                    pe.wait_ge(xt_ready, f.k + 1)
                if kc == 0 and (f.at_least(1) or q >= 2):
                    pe.wait_ge(xz_ready, f.k * XQ + (q - 1))
                ins = pe.matmul(x_bank[q % 2][:, 0:XW], x_t[f.par][:, kc, :], wx[:, kc, q * XW:(q + 1) * XW],
                                start=(kc == 0), stop=(kc == 1))
                if kc == 1:
                    ins.then_inc(xz_psum, 1)

            def down_rank(a):
                pe.wait_ge(xp_ready, a.k * 2 + 2)
                for m in both:
                    ins = pe.matmul(aux[:, 0:P], a2_w[:, m, :], xp[a.par][:, m, :], start=(m == 0), stop=(m == 1))
                ins.then_inc(u_psum, 1)

            def down_full(a, l):
                if l == 0:
                    pe.wait_ge(u_ready, a.k + 1)
                o = aux[:, l * P:(l + 1) * P]
                for m in both:
                    pe.matmul(o, down[:, m, l * P:(l + 1) * P], xp[a.par][:, m, :], start=(m == 0), stop=False)
                ins = pe.matmul(o, b2_t[:, l * P:(l + 1) * P], u_own[:, :], start=False, stop=True)
                if l == 1:
                    ins.then_inc(mid_psum, 1)

            def up_rank(a):
                pe.wait_ge(act_ready, a.k + 1)
                for l in range(2):
                    ins = pe.matmul(aux[:, 0:P], b1_w[:, l, :], act_t[:, l, :], start=(l == 0), stop=(l == 1))
                ins.then_inc(v_psum, 1)

            def up_full(a):
                if a.at_least(1):
                    pe.wait_ge(y_copied, a.k)
                pe.wait_ge(v_ready, a.k + 1)
                for m in both:
                    o = out_bank[:, m * P:(m + 1) * P]
                    for l in range(2):
                        pe.matmul(o, up_t[:, l, m * P:(m + 1) * P], act_t[:, l, :], start=(l == 0), stop=False)
                    ins = pe.matmul(o, a1_t[:, m * P:(m + 1) * P], v_own[:, :], start=False, stop=True)
                ins.then_inc(out_psum, 1)

            def transpose_y(a):
                pe.wait_ge(y_ready, a.k + 1)
                for m in both:
                    ins = pe.transpose(out_bank[:, m * P:(m + 1) * P], y_t[:, m, :], ident[:, :])
                ins.then_inc(yt_psum, 1)

            pe.wait_ge(zeroed, 1)
            for i in range(2):
                for m in both:
                    ins = pe.matmul(z_bank[i][m][:, 0:GC], zeros[:, :], zeros[:, :], start=True, stop=True)
            ins.then_inc(bits_set, 1)
            pe.wait_ge(consts_made, 5)

            pe.wait_ge(ln_step, 7)
            for i in range(2):
                ins = pe.transpose(aux[:, i * B:(i + 1) * B], c_norm[:, i * P:(i + 1) * P], ident[0:B, 0:B])
            ins.then_inc(hyp_psum, 1)
            pe.wait_ge(w_loaded["w1"], 32)
            pe.wait_ge(ln_step, 8)
            for i in range(2):
                for kc in range(2):
                    ins = pe.matmul(out_bank[:, i * B:(i + 1) * B], w1[:, kc, i * P:(i + 1) * P], c_t[:, kc, :],
                                    start=(kc == 0), stop=(kc == 1))
            ins.then_inc(hyp_psum, 1)
            pe.wait_ge(hyp_copied, 2)
            pe.wait_ge(w_loaded["b2row"], 16)
            for q in range(4):
                pe.wait_ge(w2_loaded[q % 2], 16 * (q // 2 + 1))
                if q >= 2:
                    pe.wait_ge(hyp_copied, q + 1)
                w2_r = w2[q % 2][:, :, :].rearrange("p k (d r) -> p k r d", r=RANK)
                b2_r = b2_row[:, q, :].rearrange("p (d r) -> p r d", r=RANK)
                for odd in range(2):
                    for j in range(NQ):
                        pe.matmul(x_bank[q % 2][32 * j:32 * (j + 1), 0:D], one_win[:, (1 - odd) * B:(3 - odd) * B],
                                  b2_r[:, 2 * j + odd, :], start=(odd == 0), stop=False)
                    for kc in range(2):
                        for j in range(NQ):
                            ins = pe.matmul(x_bank[q % 2][32 * j:32 * (j + 1), 0:D],
                                            hid_win[:, kc, (1 - odd) * B:(3 - odd) * B],
                                            w2_r[:, kc, 2 * j + odd, :], start=False, stop=(odd == 1 and kc == 1))
                ins.then_inc(hyp_psum, 1)
            pe.wait_ge(hyp_copied, 6)
            for n in range(2):
                for i in range(2):
                    ins = pe.transpose(x_bank[n][:, i * P:(i + 1) * P], w_tmp[:, n, i * P:(i + 1) * P],
                                       ident[:, :])
                ins.then_inc(hyp_psum, 1)
            pe.wait_ge(w_loaded["up"], 32)
            for i in range(2):
                for m in both:
                    ins = pe.transpose((out_bank, aux)[i][:, m * P:(m + 1) * P],
                                       up_raw[:, m, i * P:(i + 1) * P], ident[:, :])
                ins.then_inc(hyp_psum, 1)
            pe.wait_ge(hyp_copied, 10)

            for par in range(2):
                f = Blk(0, par)
                if par == 1:
                    pe.wait_ge(xt_ready, 1)
                transpose_x(f)
                if par == 0:
                    pe.wait_ge(wx_ready, 2 * G)
                for q in range(XQ):
                    for kc in range(2):
                        project(f, q, kc)

            pe.wait_ge(wh_ready, 2 * G)
            pe.wait_ge(down_ready, 1)

            def one_block(k, adapter, front):
                a, f = k.plus(-LAG), k.plus(2)
                for s in range(TB):
                    n = k.k * TB + (s + 1)
                    if s > 0:
                        h_prev = h_t[k.par][:, :, s - 1, 0:B]
                    elif k.at_least(1):
                        h_prev = h_t[1 - k.par][:, :, TB - 1, 0:B]
                    else:
                        h_prev = h_first[:, :, 0:B]
                    for kc in range(NM):
                        pe.wait_ge(ht_ready[kc], n)
                        for m in both:
                            if kc == 0:
                                pe.wait_ge(seeded[m], n)
                            for j in range(NQ):
                                col = (j * NM + m) * GC
                                ins = pe.matmul(z_bank[s % 2][m][32 * j:32 * j + B, 0:GC], h_prev[:, kc, :],
                                                wh[:, kc, col:col + GC], start=False, stop=(kc == 1),
                                                skip_group_check=True)
                            if kc == 1:
                                ins.then_inc(z_ready[m], 1)
                    if s == 0 and front:
                        if adapter and a.at_least(1):
                            pe.wait_ge(v_ready, a.k)
                        transpose_x(f)
                    if s == 1 and adapter and a.at_least(1):
                        transpose_y(a.plus(-1))
                    if s == 1 and adapter:
                        if front:
                            pe.wait_ge(xt_ready, f.k + 1)
                        down_rank(a)
                    if front:
                        for q, kc in {1: [(0, 0)], 2: [(0, 1), (1, 0)], 3: [(1, 1)], 4: [(2, 0)],
                                      5: [(2, 1), (3, 0)], 6: [(3, 1)]}.get(s, []):
                            project(f, q, kc)
                    if adapter:
                        if s == 3:
                            down_full(a, 0)
                        if s == 4:
                            down_full(a, 1)
                        if s == 6:
                            up_rank(a)
                        if s == 7:
                            up_full(a)

            schedule(pe, one_block)
            for t in tail:
                transpose_y(t.plus(-LAG - 1))
                if t is not tail[-1]:
                    a = t.plus(-LAG)
                    pe.wait_ge(v_ready, a.k)
                    down_rank(a)
                    down_full(a, 0)
                    down_full(a, 1)
                    up_rank(a)
                    up_full(a)

        @block.vector
        def _(dve):
            def evacuate_projection(f, q):
                dve.wait_ge(xz_psum, f.k * XQ + (q + 1))
                if q == 0 and f.at_least(1):
                    p = f.plus(-1)
                    dve.wait_ge(seed_loaded[p.par], (p.turn + 1) * (16 * NQ))
                dve.tensor_tensor(proj[:, q * XW:(q + 1) * XW], x_bank[q % 2][:, 0:XW],
                                  b_all[:, q * XW:(q + 1) * XW], ALU.add).then_inc(xz_ready, 1)

            def mask(dst, done):
                dve.tensor_tensor(dst[:, :].rearrange("p (b t) -> p b t", b=B),
                                  aux[:, 0:P].rearrange("p (b t) -> p b t", b=B),
                                  own_row[:, :].unsqueeze(2).to_broadcast([P, B, TB]), ALU.mult).then_inc(done, 1)

            def mask_u(a):
                dve.wait_ge(u_psum, a.k + 1)
                mask(u_own, u_ready)

            def mask_v(a):
                dve.wait_ge(v_psum, a.k + 1)
                mask(v_own, v_ready)

            def add_residual(a):
                dve.wait_ge(out_psum, a.k + 1)
                dve.tensor_tensor(y_t[:, :, :], xp[a.par][:, :, :],
                                  out_bank[:, 0:NM * P].rearrange("p (m t) -> p m t", m=NM), ALU.add)\
                   .then_inc(y_ready, 1)

            dve.memset(zeros[:, :], 0.0).then_inc(zeroed, 1)
            dve.memset(cond_q[:, :], 0.0).then_inc(zeroed, 1)
            dve.memset(hid_win[:, :, :], 0.0).then_inc(zeroed, 1)
            for m in both:
                dve.memset(gates[0][m][:, GC:GC + C], 0.0).then_inc(zeroed, 1)
            for i in range(2):
                dve.memset(seed[i][:, :, :], 0.0).then_inc(zeroed, 1)

            dve.wait_ge(consts_made, 2)
            dve.reduce_sum(own_row[:, :], ident[:, :].rearrange("p (r b) -> p b r", b=B), AX.X).then_inc(zeroed, 1)

            dve.wait_ge(w_loaded["cond"], 48)
            dve.reduce_sum(c_stat[:, 0:1], c_in[:, :], AX.X).then_inc(ln_step, 1)
            dve.wait_ge(ln_step, 1)
            dve.tensor_scalar(c_stat[:, 1:2], c_stat[:, 0:1], -1.0 / D, None, ALU.mult).then_inc(ln_step, 1)
            dve.wait_ge(ln_step, 2)
            dve.tensor_scalar(c_mid[:, :], c_in[:, :], c_stat[:, 1:2], None, ALU.add).then_inc(ln_step, 1)
            dve.wait_ge(ln_step, 3)
            dve.tensor_tensor(c_sq[:, :], c_mid[:, :], c_mid[:, :], ALU.mult).then_inc(ln_step, 1)
            dve.wait_ge(ln_step, 4)
            dve.reduce_sum(c_stat[:, 2:3], c_sq[:, :], AX.X).then_inc(ln_step, 1)
            dve.wait_ge(ln_step, 5)
            dve.tensor_scalar(c_stat[:, 3:4], c_stat[:, 2:3], 1.0 / D, LN_EPS, ALU.mult, ALU.add).then_inc(ln_step, 1)
            dve.wait_ge(ln_pow, 1)
            dve.scalar_tensor_tensor(c_sq[:, :], c_mid[:, :], c_stat[:, 4:5], c_gamma[:, :], ALU.mult, ALU.mult)\
               .then_inc(ln_pow, 1)
            dve.wait_ge(ln_pow, 2)
            dve.tensor_tensor(c_norm[:, :], c_sq[:, :], c_beta[:, :], ALU.add).then_inc(ln_step, 1)
            dve.wait_ge(hyp_psum, 1)
            dve.tensor_copy(c_t[:, :, :], aux[:, 0:2 * B].rearrange("p (k b) -> p k b", k=2)).then_inc(ln_step, 1)

            def reorder(dst, src, scale):
                for g in range(G):
                    yield (dst.rearrange("p (q g c) -> p g q c", g=G, c=C)[:, g],
                           src[:, g * H:(g + 1) * H].rearrange("p (q c) -> p q c", c=C),
                           scale * (2.0 if g == G - 1 else 1.0))

            for name, raw, dst, ready, whole in (("wx", wx_raw, wx, wx_ready, 1.0), ("wh", wh_raw, wh, wh_ready, 0.5)):
                dve.wait_ge(w_loaded[name], 16 * NM)
                for kc in range(NM):
                    for o, i, scale in reorder(dst[:, kc, :], raw[:, kc, :], whole):
                        dve.tensor_scalar(o, i, scale, None, ALU.mult).then_inc(ready, 1)
                if name == "wx":
                    dve.wait_ge(w_loaded["b"], 16)
                    for o, i, scale in reorder(b_all[:, :], b_raw[:, :], 1.0):
                        dve.tensor_scalar(o, i, scale, None, ALU.mult).then_inc(b_ready, 1)
            dve.wait_ge(w_loaded["down"], 16 * NM)
            dve.tensor_scalar(down[:, :, :], down_raw[:, :, :], 0.5, None, ALU.mult).then_inc(down_ready, 1)
            dve.wait_ge(w_loaded["cq"], 16 * NQ)
            dve.tensor_scalar(cond_2[:, :], cond_q[:, :], 2.0, None, ALU.mult).then_inc(cond_doubled, 1)
            dve.wait_ge(cond_doubled, 1)
            for m in both:
                dve.transpose(h_first[:, m, :], cond_2[:, m * C:(m + 1) * C]).then_inc(ht_ready[m], 1)
            dve.wait_ge(b_ready, G)
            dve.wait_ge(zeroed, 8)
            for par in range(2):
                for q in range(XQ):
                    evacuate_projection(Blk(0, par), q)

            def one_block(k, adapter, front):
                a, f = k.plus(-LAG), k.plus(2)
                for s in range(TB):
                    n = k.k * TB + (s + 1)
                    now, nxt = gates[s % 2], gates[(s + 1) % 2]
                    for m in both:
                        dve.wait_ge(gates_ready[m], n)
                        dve.scalar_tensor_tensor(prod[m][:, :], now[m][:, 0:2 * C], 1.0, now[m][:, 3 * C:5 * C],
                                                 ALU.add, ALU.mult).then_inc(prod_ready[m], 1)
                        dve.wait_ge(prod_ready[m], n)
                        dve.scalar_tensor_tensor(nxt[m][:, GC:GC + C], prod[m][:, C:2 * C], 0.5, prod[m][:, 0:C],
                                                 ALU.mult, ALU.add).then_inc(cell_ready[m], 1)
                    for m in both:
                        dve.wait_ge(tanc_ready[m], n)
                        dve.scalar_tensor_tensor(hid[m][:, :], now[m][:, 2 * C:3 * C], 1.0, tanc[m][:, :],
                                                 ALU.add, ALU.mult).then_inc(hid_ready[m], 1)
                        if s == 0 and m == 0 and k.at_least(2):
                            dve.wait_ge(xp_ready, k.k * 2 - 2)
                        dve.wait_ge(hid_ready[m], n)
                        dve.transpose(h_t[k.par][:, m, s, :], hid[m][:, :]).then_inc(ht_ready[m], 1)
                    if s == 1 and adapter:
                        mask_u(a)
                    if s in (2, 3) and front:
                        evacuate_projection(f, s - 2)
                    if s in (5, 6) and front:
                        evacuate_projection(f, s - 3)
                    if s == 6 and adapter:
                        mask_v(a)
                    if s == 7 and adapter:
                        add_residual(a)

            schedule(dve, one_block)
            for t in tail[:-1]:
                a = t.plus(-LAG)
                mask_u(a)
                mask_v(a)
                add_residual(a)

        @block.gpsimd
        def _(pool):
            pool.memset(ident[:, :], 0.0).then_inc(consts_made, 1)
            pool.wait_ge(consts_made, 1)
            pool.affine_select(out=ident[:, :], in_=ident[:, :], compare_op=ALU.not_equal, fill=1.0, base=0,
                               pattern=[[-1, P]], channel_multiplier=1).then_inc(consts_made, 1)
            pool.memset(neg_half[:, :], -0.5).then_inc(consts_made, 1)
            pool.memset(one_win[:, :], 0.0).then_inc(consts_made, 1)
            pool.wait_ge(consts_made, 4)
            pool.memset(one_win[:, B:2 * B], 1.0).then_inc(consts_made, 1)
            pool.dma_start(b2_row[:, :, :], bias2.rearrange("(a q n) -> a q n", a=1, q=4)).then_inc(w_loaded["b2row"], 16)
            pool.wait_ge(ln_step, 6)
            pool.tensor_tensor(c_stat[:, 4:5], c_stat[:, 3:4], neg_half[:, :], ALU.pow).then_inc(ln_pow, 1)

            def permute_x(f):
                pool.wait_ge(x_loaded[f.par], (f.turn + 1) * 16)
                if f.at_least(2):
                    pool.wait_ge(xt_psum, f.k - 1)
                natural = perm(x_nat[f.par][:, :])
                pool.tensor_tensor(x_perm[f.par][:, :].rearrange("p (m j c) -> p m j c", m=NM, j=NQ),
                                   natural, natural, ALU.add).then_inc(x_permuted, 1)

            def keep_x(f):
                pool.wait_ge(xt_ready, f.k + 1)
                if f.at_least(2):
                    pool.wait_ge(xp_ready, f.k * 2 - 2)
                pool.tensor_tensor(x_keep[f.par][:, :, :], x_t[f.par][:, :, :], x_t[f.par][:, :, :], ALU.add)\
                    .then_inc(x_kept, 1)

            def add_h(k):
                pool.wait_ge(x_kept, k.k + 1)
                if k.at_least(2):
                    pool.wait_ge(y_ready, k.k - 1)
                for m in both:
                    pool.wait_ge(ht_ready[m], k.k * TB + (TB + 1))
                    tokens = "p (b t) -> p b t"
                    pool.tensor_tensor(xp[k.par][:, m, :].rearrange(tokens, b=B),
                                       x_keep[k.par][:, m, :].rearrange(tokens, b=B),
                                       h_t[k.par][:, m, :, 0:B].rearrange("p t b -> p b t"), ALU.add)\
                        .then_inc(xp_ready, 1)

            for par in range(3):
                permute_x(Blk(0, 0, par))
            for par in range(2):
                keep_x(Blk(0, par))

            def one_block(k, adapter, front):
                if k.plus(3).exists():
                    permute_x(k.plus(3))
                add_h(k)
                if front:
                    keep_x(k.plus(2))

            schedule(pool, one_block, 2)


_INS = ["x", "cond_1024", "L0_cond_Wx", "L0_cond_Wh", "L0_cond_b", "L1_cond_base_up", "L1_cond_base_down",
        "L1_cond_ln_gamma", "L1_cond_ln_beta", "L1_cond_W1", "L1_cond_bias1", "L1_cond_W2", "L1_cond_bias2"]


def kernel(**inputs):
    import numpy as _np
    import concourse.bacc as _bacc
    from concourse import mybir as _mybir
    from concourse.bass_utils import run_bass_kernel_spmd as _run

    nc = _bacc.Bacc("TRN2", target_bir_lowering=False, num_devices=1)
    arrays, args = {}, []
    for name in _INS:
        a = _np.ascontiguousarray(inputs[name])
        arrays[f"in_{name}"] = a
        args.append(nc.dram_tensor(f"in_{name}", a.shape, _mybir.dt.from_np(a.dtype), kind="ExternalInput").ap())
    args.append(nc.dram_tensor("out_0", (B, T, D), F32, kind="ExternalOutput").ap())
    lstm_adapter(nc, *args)
    r = _run(nc, [arrays], core_ids=[0])
    return r.results[0]["out_0"]
```

```python
from contextlib import ExitStack

import concourse.bass as bass
from concourse import mybir

F32 = mybir.dt.float32
ALU = mybir.AluOpType
ACT = mybir.ActivationFunctionType
AX = mybir.AxisListType

B, T, D, H = 16, 256, 256, 256
G = 4
P = 128
NQ, NM, C = 4, 2, 32
TB = 8
NBLK = T // TB
RANK = 8
GC = 3 * C
OC = NM * C
ZW = NM * GC + OC
XQ = 4
XW = G * H // XQ
LN_EPS = 1e-5
QUARTERS = (1, 2, 0, 3)
W_STEPS = 6
EARLY = 3
PEELED = 3


def lstm_adapter(nc, x, cond, Wx, Wh, b, base_up, base_down, gamma, beta, W1, bias1, W2, bias2, out):
    ctx = ExitStack()
    with ctx:
        def sb(name, shape):
            return ctx.enter_context(nc.sbuf_tensor(name, shape, F32))

        def psum(name):
            return ctx.enter_context(nc.psum_tensor(name, [P, 512], F32))

        def sem(name):
            return ctx.enter_context(nc.semaphore(name))

        ident = sb("ident", [P, P])
        zeros = sb("zeros", [P, P])
        one_win = sb("one_win", [1, 3 * B])
        own_row = sb("own_row", [P, B])
        neg_half = sb("neg_half", [B, 1])
        wx_raw = sb("wx_raw", [P, NM, G * H])
        wh_raw = sb("wh_raw", [P, NM, G * H])
        b_raw = sb("b_raw", [P, G * H])
        wx = sb("wx", [P, NM, G * H])
        wh = sb("wh", [P, NM, G * H])
        b_all = sb("b_all", [P, G * H])
        down_raw = sb("down_raw", [P, NM, D])
        down = sb("down", [P, NM, D])
        up_raw = sb("up_raw", [P, NM, D])
        up_t = sb("up_t", [P, 2, D])
        a1_t = sb("a1_t", [P, D])
        b2_t = sb("b2_t", [P, D])
        b1_w = sb("b1_w", [P, 2, P])
        a2_w = sb("a2_w", [P, NM, P])
        c_in = sb("c_in", [B, D])
        c_gamma = sb("c_gamma", [B, D])
        c_beta = sb("c_beta", [B, D])
        c_mid = sb("c_mid", [B, D])
        c_sq = sb("c_sq", [B, D])
        c_norm = sb("c_norm", [B, D])
        c_stat = sb("c_stat", [B, 5])
        c_t = sb("c_t", [P, 2, B])
        w1 = sb("w1", [P, 2, D])
        b1_col = sb("b1_col", [P, 2])
        hid_win = sb("hid_win", [P, 2, 3 * B])
        w2_tiles = [sb(f"w2_{n}", [P, 2, D * RANK]) for n in range(3)]
        w2 = {q: w2_tiles[n % 3] for n, q in enumerate(QUARTERS)}
        b2_row = sb("b2_row", [1, 4, D * RANK])
        w_tmp = sb("w_tmp", [P, 2, D])
        x_nat = [sb(f"x_nat{i}", [P, D]) for i in range(2)]
        x_perm = [sb(f"x_perm{i}", [P, D]) for i in range(2)]
        x_t = [sb(f"x_t{i}", [P, NM, P]) for i in range(2)]
        x_keep = [sb(f"x_keep{i}", [P, NM, P]) for i in range(2)]
        proj = sb("proj", [P, G * H])
        seed = [sb(f"seed{i}", [P, TB, ZW]) for i in range(2)]
        cond_q = sb("cond_q", [P, NM * C])
        cond_2 = sb("cond_2", [P, NM * C])
        h_first = sb("h_first", [P, NM, 32])
        gates = [[sb(f"gates{i}_{m}", [P, GC + C]) for m in range(NM)] for i in range(2)]
        gate_o = sb("gate_o", [P, OC])
        prod = [sb(f"prod{m}", [P, 2 * C]) for m in range(NM)]
        tanc = [sb(f"tanc{m}", [P, C]) for m in range(NM)]
        hid = [sb(f"hid{m}", [P, C]) for m in range(NM)]
        h_t = [sb(f"h_t{i}", [P, NM, TB, 32]) for i in range(2)]
        xp = [sb(f"xp{i}", [P, NM, P]) for i in range(2)]
        xp_early = [sb(f"xp_early{i}", [P, NM, P]) for i in range(EARLY)]
        lanes = range(2)
        u_own = [sb(f"u_own{i}", [P, P]) for i in lanes]
        v_own = [sb(f"v_own{i}", [P, P]) for i in lanes]
        act_t = [sb(f"act_t{i}", [P, 2, P]) for i in lanes]
        y_t = [sb(f"y_t{i}", [P, NM, P]) for i in lanes]
        y_nat = [[sb(f"y_nat{lane}_{i}", [P, D]) for i in range(2)] for lane in lanes]

        z_bank = [psum(f"z{m}") for m in range(NM)]
        o_bank = psum("z_o")
        aux = psum("aux")
        out_bank = psum("out_bank")
        x_bank = [psum(f"x_bank{i}") for i in range(2)]
        mid_bank, up_bank = (aux, x_bank[0]), (out_bank, x_bank[1])

        consts_made = sem("consts_made")
        zeroed = sem("zeroed")
        w_loaded = {n: sem(f"{n}_loaded") for n in
                    ("wx", "wh", "b", "down", "up", "cond", "cq", "w1", "b2row")}
        w2_loaded = [sem(f"w2_loaded{q}") for q in range(4)]
        wx_ready, wh_ready = sem("wx_ready"), sem("wh_ready")
        b_ready, down_ready = sem("b_ready"), sem("down_ready")
        bits_set = sem("bits_set")
        cond_doubled = sem("cond_doubled")
        ln_step, ln_pow = sem("ln_step"), sem("ln_pow")
        cond_t_psum, cond_t_ready = sem("cond_t_psum"), sem("cond_t_ready")
        hidden_psum, hidden_ready = sem("hidden_psum"), sem("hidden_ready")
        up_psum, up_ready = sem("up_psum"), sem("up_ready")
        w_psum, w_copied = sem("w_psum"), sem("w_copied")
        wt_psum, wt_ready = sem("wt_psum"), sem("wt_ready")
        x_loaded = [sem(f"x_loaded{i}") for i in range(2)]
        x_permuted = sem("x_permuted")
        xt_psum, xt_ready = sem("xt_psum"), sem("xt_ready")
        x_kept = sem("x_kept")
        xz_psum, xz_ready = sem("xz_psum"), sem("xz_ready")
        seed_loaded = [sem(f"seed_loaded{i}") for i in range(2)]
        both = range(NM)
        seeded = [sem(f"seeded{m}") for m in both]
        seeded_o, zo_ready, gate_o_ready = sem("seeded_o"), sem("zo_ready"), sem("gate_o_ready")
        z_ready = [sem(f"z_ready{m}") for m in both]
        gates_ready = [sem(f"gates_ready{m}") for m in both]
        prod_ready = [sem(f"prod_ready{m}") for m in both]
        cell_ready = [sem(f"cell_ready{m}") for m in both]
        tanc_ready = [sem(f"tanc_ready{m}") for m in both]
        hid_ready = [sem(f"hid_ready{m}") for m in both]
        ht_ready = [sem(f"ht_ready{m}") for m in both]
        xp_ready = sem("xp_ready")
        u_psum, u_ready = ([sem(f"{n}{i}") for i in lanes] for n in ("u_psum", "u_ready"))
        mid_psum, act_ready = ([sem(f"{n}{i}") for i in lanes] for n in ("mid_psum", "act_ready"))
        v_psum, v_ready = ([sem(f"{n}{i}") for i in lanes] for n in ("v_psum", "v_ready"))
        out_psum, y_ready = ([sem(f"{n}{i}") for i in lanes] for n in ("out_psum", "y_ready"))
        yt_psum, y_copied = ([sem(f"{n}{i}") for i in lanes] for n in ("yt_psum", "y_copied"))
        stored = [[sem(f"stored{lane}_{i}") for i in range(2)] for lane in lanes]

        block = ctx.enter_context(nc.Block())

        def perm(ap):
            return ap.rearrange("p (j m c) -> p m j c", j=NQ, m=NM)

        class Blk:

            def __init__(self, it, par, shift=0):
                self.k = it * 2 + (par + shift)
                self.par = (par + shift) % 2
                self.turn = it + (par + shift) // 2
                self.it, self.p, self.s = it, par, shift

            def plus(self, n):
                return Blk(self.it, self.p, self.s + n)

            def at_least(self, n):
                return not isinstance(self.k, int) or self.k >= n

            def exists(self):
                return not isinstance(self.k, int) or 0 <= self.k < NBLK

        def schedule(eng, one_block, last=1):
            for pair in range(PEELED):
                for par in range(2):
                    one_block(Blk(pair, par), True)
            with eng.Fori(PEELED, NBLK // 2 - last) as it:
                for par in range(2):
                    one_block(Blk(it, par), True)
            for pair in range(NBLK // 2 - last, NBLK // 2):
                for par in range(2):
                    one_block(Blk(pair, par), pair < NBLK // 2 - 1)

        class Job:

            def __init__(self, blk, lane):
                self.blk, self.lane = blk, lane
                self.seq = blk.plus(-EARLY) if lane == 0 else blk
                self.xp = xp[blk.par] if lane == 0 else xp_early[blk.k]

        def follower(k):
            return Job(k.plus(-1), 0) if k.at_least(EARLY + 1) else None

        def early(k):
            n = k.k - (NBLK - 2) if isinstance(k.k, int) else -1
            return Job(Blk(0, 0, n), 1) if 0 <= n < EARLY else None

        end = Blk(NBLK // 2, 0)
        last_jobs = (follower(end), early(end))

        @block.sync
        def _(sp):
            def load_x(f):
                first = f.k * TB if isinstance(f.k, int) else sp.snap(f.k * TB)
                if f.at_least(2):
                    sp.wait_ge(x_permuted, f.k - 1)
                sp.dma_start(x_nat[f.par][:, :], x[:, bass.ds(first, TB), :]).then_inc(x_loaded[f.par], 16)

            def load_seed(f):
                consumed = f.k * TB - TB if isinstance(f.k, int) else sp.snap(f.k * TB - TB)
                if f.at_least(2):
                    for m in both:
                        sp.wait_ge(seeded[m], consumed)
                sp.wait_ge(xz_ready, f.k * XQ + XQ)
                for j in range(NQ):
                    sp.dma_start(seed[f.par][32 * j:32 * j + B, :, :], proj[:, ZW * j:ZW * (j + 1)])\
                      .then_inc(seed_loaded[f.par], 16)

            def store_y(a):
                first = a.blk.k * TB if isinstance(a.blk.k, int) else sp.snap(a.blk.k * TB)
                sp.wait_ge(y_copied[a.lane], a.seq.k + 1)
                sp.dma_start(out[:, bass.ds(first, TB), :], y_nat[a.lane][a.seq.par][:, :])\
                  .then_inc(stored[a.lane][a.seq.par], 16)

            by_half = "(j m c) n -> m j c n"

            def load_halves(dst, src, name):
                for m in both:
                    sp.dma_start(dst[:, m, :], src.rearrange(by_half, j=NQ, m=NM)[m]).then_inc(w_loaded[name], 16)

            w2_q = W2.rearrange("(k p) (q n) -> q p k n", p=P, q=4)

            def load_w2(q):
                sp.dma_start(w2[q][:, :, :], w2_q[q]).then_inc(w2_loaded[q], 16)

            load_x(Blk(0, 0))
            load_halves(wx_raw, Wx, "wx")
            load_x(Blk(0, 1))
            sp.dma_start(b_raw[:, :], b.partition_broadcast(P)).then_inc(w_loaded["b"], 16)
            load_halves(wh_raw, Wh, "wh")
            load_seed(Blk(0, 0))
            load_x(Blk(0, 0, 2))
            sp.dma_start(w1[:, :, :], W1.rearrange("(k p) n -> p k n", p=P)).then_inc(w_loaded["w1"], 16)
            sp.dma_start(b1_col[:, :], bias1.rearrange("(k p) -> p k", p=P),
                         allow_slow_non_contiguous=True).then_inc(w_loaded["w1"], 16)
            load_w2(QUARTERS[0])
            load_seed(Blk(0, 1))
            load_halves(up_raw, base_up, "up")
            load_halves(down_raw, base_down, "down")
            for q in QUARTERS[1:3]:
                load_w2(q)

            def one_block(k, front):
                if k.plus(3).exists():
                    load_x(k.plus(3))
                if front:
                    load_seed(k.plus(2))
                if not k.at_least(2) and k.k == 1:
                    sp.wait_ge(w_psum, 1)
                    load_w2(QUARTERS[3])
                done = follower(k.plus(-1))
                if done and done.seq.exists():
                    store_y(done)
                if early(k):
                    store_y(early(k))

            schedule(sp, one_block, 2)
            store_y(follower(Blk(NBLK // 2 - 1, 1)))
            for a in last_jobs:
                store_y(a)
            for lane, jobs in enumerate((NBLK - EARLY, EARLY)):
                for i in range(2):
                    sp.wait_ge(stored[lane][i], 16 * ((jobs + 1 - i) // 2))

        @block.scalar
        def _(act):
            act.wait_ge(zeroed, 1)
            for j in range(NQ):
                act.dma_start(cond_q[32 * j:32 * j + B, :], cond[:, NM * C * j:NM * C * (j + 1)])\
                   .then_inc(w_loaded["cq"], 16)

            def evacuate_x(f):
                act.wait_ge(xt_psum, f.k + 1)
                if f.at_least(2):
                    act.wait_ge(xz_psum, (f.k - 1) * XQ)
                    act.wait_ge(x_kept, f.k - 1)
                act.activation(x_t[f.par][:, :, :], aux[:, 0:NM * P].rearrange("p (m t) -> p m t", m=NM),
                               ACT.Copy, scale=0.5).then_inc(xt_ready, 1)

            def seed_bank(buf, s, m):
                act.activation(z_bank[m][:, 0:GC], seed[buf][:, s, GC * m:GC * (m + 1)], ACT.Copy)\
                   .then_inc(seeded[m], 1)

            def seed_o(buf, s):
                act.activation(o_bank[:, 0:OC], seed[buf][:, s, NM * GC:ZW], ACT.Copy).then_inc(seeded_o, 1)

            def gelu_mid(a):
                act.wait_ge(mid_psum[a.lane], a.seq.k + 1)
                if a.seq.at_least(1):
                    act.wait_ge(out_psum[a.lane], a.seq.k)
                act.activation(act_t[a.lane][:, :, :],
                               mid_bank[a.lane][:, 0:2 * P].rearrange("p (l t) -> p l t", l=2),
                               ACT.Gelu).then_inc(act_ready[a.lane], 1)

            def copy_y(a):
                act.wait_ge(yt_psum[a.lane], a.seq.k + 1)
                if a.seq.at_least(2):
                    act.wait_ge(stored[a.lane][a.seq.par], a.seq.turn * 16)
                act.activation(perm(y_nat[a.lane][a.seq.par][:, :]),
                               up_bank[a.lane][:, 0:D].rearrange("p (m j c) -> p m j c", m=NM, j=NQ),
                               ACT.Copy).then_inc(y_copied[a.lane], 1)

            def make_weights(k, s):
                if k == 0 and s == 2:
                    act.wait_ge(w_loaded["w1"], 32)
                    act.wait_ge(hidden_psum, 1)
                    for i in range(2):
                        act.activation(hid_win[:, i, B:2 * B], aux[:, i * B:(i + 1) * B], ACT.Gelu,
                                       bias=b1_col[:, i:i + 1]).then_inc(hidden_ready, 1)
                if k == 0 and s in (4, 5):
                    act.wait_ge(up_psum, s - 3)
                    act.activation(up_t[:, s - 4, :], out_bank[:, 0:D], ACT.Copy).then_inc(up_ready, 1)
                if k >= 1 and ((k - 1) * TB + s) % W_STEPS == W_STEPS - 1:
                    n = ((k - 1) * TB + s) // W_STEPS
                    q = QUARTERS[n]
                    act.wait_ge(w_psum, n + 1)
                    src = out_bank[:, 0:D]
                    if q == 0:
                        ins = act.activation(a1_t[:, :].rearrange("p (m j c) -> p m j c", m=NM, j=NQ), perm(src),
                                             ACT.Copy)
                    elif q == 1:
                        ins = act.activation(w_tmp[:, 0, :], src, ACT.Copy)
                    elif q == 2:
                        ins = act.activation(w_tmp[:, 1, :].rearrange("p (m j c) -> p m j c", m=NM, j=NQ), perm(src),
                                             ACT.Copy, scale=0.5)
                    else:
                        ins = act.activation(b2_t[:, :], src, ACT.Copy)
                    ins.then_inc(w_copied, 1)
                if k == 2 and s in (2, 6):
                    n = s // 4
                    act.wait_ge(wt_psum, n + 1)
                    act.activation((b1_w, a2_w)[n][:, :, :], aux[:, 0:2 * P].rearrange("p (l t) -> p l t", l=2),
                                   ACT.Copy).then_inc(wt_ready, 1)

            for par in range(2):
                evacuate_x(Blk(0, par))
            act.wait_ge(bits_set, 1)
            act.wait_ge(seed_loaded[0], 16 * NQ)
            for m in both:
                seed_bank(0, 0, m)
            seed_o(0, 0)

            def one_block(k, front):
                a, e, done = follower(k), early(k), follower(k.plus(-1))
                for s in range(TB):
                    n = k.k * TB + (s + 1)
                    more = s < TB - 1 or front or k.p == 0
                    ahead, s_next = (k, s + 1) if s < TB - 1 else (k.plus(1), 0)

                    def gates_of(m):
                        act.wait_ge(z_ready[m], n)
                        act.activation(gates[s % 2][m][:, 0:GC], z_bank[m][:, 0:GC], ACT.Tanh,
                                       scale=0.5).then_inc(gates_ready[m], 1)

                    def tanh_cell(m):
                        act.wait_ge(cell_ready[m], n)
                        act.activation(tanc[m][:, :], gates[(s + 1) % 2][m][:, GC:GC + C], ACT.Tanh,
                                       scale=0.5).then_inc(tanc_ready[m], 1)

                    if s == TB - 1 and more:
                        act.wait_ge(seed_loaded[ahead.par], (ahead.turn + 1) * (16 * NQ))
                    gates_of(0)
                    gates_of(1)
                    act.wait_ge(zo_ready, n)
                    act.activation(gate_o[:, :], o_bank[:, 0:OC], ACT.Tanh, scale=0.5).then_inc(gate_o_ready, 1)
                    tanh_cell(0)
                    if more:
                        act.wait_ge(gates_ready[0], n)
                        seed_bank(ahead.par, s_next, 0)
                    tanh_cell(1)
                    if more:
                        act.wait_ge(gates_ready[1], n)
                        seed_bank(ahead.par, s_next, 1)
                        act.wait_ge(gate_o_ready, n)
                        seed_o(ahead.par, s_next)
                    if s == 0 and front:
                        evacuate_x(k.plus(2))
                    if not k.at_least(EARLY + 1):
                        make_weights(k.k, s)
                    if s == 1 and done and done.seq.exists():
                        copy_y(done)
                    if s == 2 and e:
                        gelu_mid(e)
                    if s == 4 and a:
                        gelu_mid(a)
                    if s == 6 and e:
                        copy_y(e)

            schedule(act, one_block)
            copy_y(follower(Blk(NBLK // 2 - 1, 1)))
            for a in last_jobs:
                gelu_mid(a)
            for a in last_jobs:
                copy_y(a)

        @block.tensor
        def _(pe):
            def transpose_x(f):
                pe.wait_ge(x_permuted, f.k + 1)
                for m in both:
                    ins = pe.transpose(aux[:, m * P:(m + 1) * P], x_perm[f.par][:, m * P:(m + 1) * P], ident[:, :])
                ins.then_inc(xt_psum, 1)

            def project(f, q, kc):
                if q == 0 and kc == 0:
                    pe.wait_ge(xt_ready, f.k + 1)
                if kc == 0 and (f.at_least(1) or q >= 2):
                    pe.wait_ge(xz_ready, f.k * XQ + (q - 1))
                ins = pe.matmul(x_bank[q % 2][:, 0:XW], x_t[f.par][:, kc, :], wx[:, kc, q * XW:(q + 1) * XW],
                                start=(kc == 0), stop=(kc == 1))
                if kc == 1:
                    ins.then_inc(xz_psum, 1)

            def down_rank(a):
                if a.lane == 0 and a.seq.at_least(1):
                    pe.wait_ge(v_ready[0], a.seq.k)
                pe.wait_ge(wt_ready, 2)
                pe.wait_ge(xp_ready, a.blk.k * 2 + 2)
                for m in both:
                    ins = pe.matmul(mid_bank[a.lane][:, 0:P], a2_w[:, m, :], a.xp[:, m, :],
                                    start=(m == 0), stop=(m == 1))
                ins.then_inc(u_psum[a.lane], 1)

            def down_full(a, l):
                if l == 0:
                    pe.wait_ge(w_copied, 4)
                    pe.wait_ge(down_ready, 1)
                    pe.wait_ge(u_ready[a.lane], a.seq.k + 1)
                o = mid_bank[a.lane][:, l * P:(l + 1) * P]
                for m in both:
                    pe.matmul(o, down[:, m, l * P:(l + 1) * P], a.xp[:, m, :], start=(m == 0), stop=False)
                ins = pe.matmul(o, b2_t[:, l * P:(l + 1) * P], u_own[a.lane][:, :], start=False, stop=True)
                if l == 1:
                    ins.then_inc(mid_psum[a.lane], 1)

            def up_rank(a):
                pe.wait_ge(act_ready[a.lane], a.seq.k + 1)
                for l in range(2):
                    ins = pe.matmul(mid_bank[a.lane][:, 0:P], b1_w[:, l, :], act_t[a.lane][:, l, :],
                                    start=(l == 0), stop=(l == 1))
                ins.then_inc(v_psum[a.lane], 1)

            def up_full(a, m):
                if m == 0:
                    if a.seq.at_least(1):
                        pe.wait_ge(y_copied[a.lane], a.seq.k)
                    pe.wait_ge(up_ready, 2)
                    pe.wait_ge(v_ready[a.lane], a.seq.k + 1)
                o = up_bank[a.lane][:, m * P:(m + 1) * P]
                for l in range(2):
                    pe.matmul(o, up_t[:, l, m * P:(m + 1) * P], act_t[a.lane][:, l, :], start=(l == 0), stop=False)
                ins = pe.matmul(o, a1_t[:, m * P:(m + 1) * P], v_own[a.lane][:, :], start=False, stop=True)
                if m == 1:
                    ins.then_inc(out_psum[a.lane], 1)

            def transpose_y(a):
                pe.wait_ge(y_ready[a.lane], a.seq.k + 1)
                for m in both:
                    ins = pe.transpose(up_bank[a.lane][:, m * P:(m + 1) * P], y_t[a.lane][:, m, :], ident[:, :])
                ins.then_inc(yt_psum[a.lane], 1)

            def make_weights(k, s):
                if k == 0 and s == 1:
                    pe.wait_ge(ln_step, 7)
                    pe.wait_ge(xt_ready, 3)
                    for i in range(2):
                        ins = pe.transpose(aux[:, i * B:(i + 1) * B], c_norm[:, i * P:(i + 1) * P], ident[0:B, 0:B])
                    ins.then_inc(cond_t_psum, 1)
                if k == 0 and s == 2:
                    pe.wait_ge(w_loaded["w1"], 32)
                    pe.wait_ge(cond_t_ready, 1)
                    for i in range(2):
                        for kc in range(2):
                            ins = pe.matmul(aux[:, i * B:(i + 1) * B], w1[:, kc, i * P:(i + 1) * P], c_t[:, kc, :],
                                            start=(kc == 0), stop=(kc == 1))
                    ins.then_inc(hidden_psum, 1)
                if k == 0 and s in (4, 5):
                    if s == 4:
                        pe.wait_ge(w_loaded["up"], 32)
                    else:
                        pe.wait_ge(up_ready, 1)
                    for m in both:
                        ins = pe.transpose(out_bank[:, m * P:(m + 1) * P], up_raw[:, m, (s - 4) * P:(s - 3) * P],
                                           ident[:, :])
                    ins.then_inc(up_psum, 1)
                if k >= 1:
                    n, i = divmod((k - 1) * TB + s, W_STEPS)
                    q, odd, part = QUARTERS[n], i // 3, i % 3
                    if n == 0 and i == 0:
                        pe.wait_ge(w_loaded["b2row"], 16)
                        pe.wait_ge(hidden_ready, 2)
                        pe.wait_ge(up_ready, 2)
                    elif i == 0:
                        pe.wait_ge(w_copied, n)
                    if i == 1:
                        pe.wait_ge(w2_loaded[q], 16)
                    window = slice((1 - odd) * B, (3 - odd) * B)
                    for j in range(NQ):
                        r = 2 * j + odd
                        if part == 0:
                            lhs, rhs = one_win[:, window], b2_row[:, q, :].rearrange("p (d r) -> p r d", r=RANK)[:, r, :]
                        else:
                            lhs = hid_win[:, part - 1, window]
                            rhs = w2[q][:, part - 1, :].rearrange("p (d r) -> p r d", r=RANK)[:, r, :]
                        ins = pe.matmul(out_bank[32 * j:32 * (j + 1), 0:D], lhs, rhs, start=(i == 0),
                                        stop=(i == W_STEPS - 1))
                    if i == W_STEPS - 1:
                        ins.then_inc(w_psum, 1)
                if k == 2 and s in (2, 6):
                    n = s // 4
                    pe.wait_ge(w_copied, n + 1)
                    if n == 0:
                        pe.wait_ge(xt_ready, k + 3)
                    else:
                        pe.wait_ge(wt_ready, 1)
                    for i in range(2):
                        ins = pe.transpose(aux[:, i * P:(i + 1) * P], w_tmp[:, n, i * P:(i + 1) * P], ident[:, :])
                    ins.then_inc(wt_psum, 1)

            pe.wait_ge(zeroed, 2)
            for bank in (*z_bank, o_bank):
                ins = pe.matmul(bank[:, 0:GC], zeros[:, :], zeros[:, 0:GC], start=True, stop=True)
            ins.then_inc(bits_set, 1)
            pe.wait_ge(consts_made, 5)

            for par in range(2):
                f = Blk(0, par)
                if par == 1:
                    pe.wait_ge(xt_ready, 1)
                transpose_x(f)
                if par == 0:
                    pe.wait_ge(wx_ready, 2 * G)
                for q in range(XQ):
                    for kc in range(2):
                        project(f, q, kc)

            pe.wait_ge(wh_ready, 2 * G)

            def one_block(k, front):
                a, e, done, f = follower(k), early(k), follower(k.plus(-1)), k.plus(2)
                for s in range(TB):
                    n = k.k * TB + (s + 1)
                    if s > 0:
                        h_prev = h_t[k.par][:, :, s - 1, 0:B]
                    elif k.at_least(1):
                        h_prev = h_t[1 - k.par][:, :, TB - 1, 0:B]
                    else:
                        h_prev = h_first[:, :, 0:B]
                    order = ((0, 0), (1, 0), (0, 1), (1, 1)) if s % 2 == 0 else ((0, 0), (0, 1), (1, 0), (1, 1))
                    for i, (kc, m) in enumerate(order + ((0, NM), (1, NM))):
                        if kc not in [o[0] for o in order[:i]]:
                            pe.wait_ge(ht_ready[kc], n)
                        if kc == 0:
                            pe.wait_ge(seeded[m] if m < NM else seeded_o, n)
                        bank, width = (z_bank[m], GC) if m < NM else (o_bank, OC)
                        for j in range(NQ):
                            col = j * ZW + m * GC
                            ins = pe.matmul(bank[32 * j:32 * j + B, 0:width], h_prev[:, kc, :],
                                            wh[:, kc, col:col + width], start=False, stop=(kc == 1),
                                            skip_group_check=True)
                        if kc == 1:
                            ins.then_inc(z_ready[m] if m < NM else zo_ready, 1)
                    if s == 0 and front:
                        if done and done.seq.exists():
                            pe.wait_ge(v_ready[0], a.seq.k)
                        elif k.k == EARLY:
                            pe.wait_ge(wt_ready, 2)
                        transpose_x(f)
                    if s == 1 and done and done.seq.exists():
                        transpose_y(done)
                    if s == 1 and a:
                        if front:
                            pe.wait_ge(xt_ready, f.k + 1)
                        down_rank(a)
                    if front:
                        for q, kc in {1: [(0, 0)], 2: [(0, 1), (1, 0)], 3: [(1, 1)], 4: [(2, 0)],
                                      5: [(2, 1)], 6: [(3, 0)], 7: [(3, 1)]}.get(s, []):
                            project(f, q, kc)
                    if not k.at_least(EARLY + 1):
                        make_weights(k.k, s)
                    if a:
                        if s in (3, 4):
                            down_full(a, s - 3)
                        if s == 5:
                            up_rank(a)
                        if s in (6, 7):
                            up_full(a, s - 6)
                    if e:
                        if s == 0:
                            pe.wait_ge(xz_ready, NBLK * XQ)
                            down_rank(e)
                        if s in (1, 2):
                            down_full(e, s - 1)
                        if s == 3:
                            up_rank(e)
                        if s in (4, 5):
                            up_full(e, s - 4)
                        if s == 6:
                            transpose_y(e)

            schedule(pe, one_block)
            transpose_y(follower(Blk(NBLK // 2 - 1, 1)))
            for a in last_jobs:
                if a.lane == 1:
                    pe.wait_ge(v_ready[1], a.seq.k)
                down_rank(a)
            for a in last_jobs:
                for l in range(2):
                    down_full(a, l)
            for a in last_jobs:
                up_rank(a)
            for a in last_jobs:
                for m in both:
                    up_full(a, m)
            for a in last_jobs:
                transpose_y(a)

        @block.vector
        def _(dve):
            def evacuate_projection(f, q):
                dve.wait_ge(xz_psum, f.k * XQ + (q + 1))
                if q == 0 and f.at_least(1):
                    p = f.plus(-1)
                    dve.wait_ge(seed_loaded[p.par], (p.turn + 1) * (16 * NQ))
                dve.tensor_tensor(proj[:, q * XW:(q + 1) * XW], x_bank[q % 2][:, 0:XW],
                                  b_all[:, q * XW:(q + 1) * XW], ALU.add).then_inc(xz_ready, 1)

            def mask(bank, dst, done):
                dve.tensor_tensor(dst[:, :].rearrange("p (b t) -> p b t", b=B),
                                  bank[:, 0:P].rearrange("p (b t) -> p b t", b=B),
                                  own_row[:, :].unsqueeze(2).to_broadcast([P, B, TB]), ALU.mult).then_inc(done, 1)

            def mask_u(a):
                dve.wait_ge(u_psum[a.lane], a.seq.k + 1)
                mask(mid_bank[a.lane], u_own[a.lane], u_ready[a.lane])

            def mask_v(a):
                dve.wait_ge(v_psum[a.lane], a.seq.k + 1)
                mask(mid_bank[a.lane], v_own[a.lane], v_ready[a.lane])

            def add_residual(a):
                dve.wait_ge(out_psum[a.lane], a.seq.k + 1)
                dve.tensor_tensor(y_t[a.lane][:, :, :], a.xp[:, :, :],
                                  up_bank[a.lane][:, 0:NM * P].rearrange("p (m t) -> p m t", m=NM), ALU.add)\
                   .then_inc(y_ready[a.lane], 1)

            dve.memset(cond_q[:, :], 0.0).then_inc(zeroed, 1)
            dve.memset(zeros[:, :], 0.0).then_inc(zeroed, 1)
            dve.memset(hid_win[:, :, :], 0.0).then_inc(zeroed, 1)
            for m in both:
                dve.memset(gates[0][m][:, GC:GC + C], 0.0).then_inc(zeroed, 1)
            for i in range(2):
                dve.memset(seed[i][:, :, :], 0.0).then_inc(zeroed, 1)

            def reorder(dst, src, scale):
                quadrants = dst.rearrange("p (j n) -> p j n", n=ZW)
                for g in range(G):
                    place = {0: 0, 1: 1, 3: 2}.get(g)
                    if place is None:
                        o = quadrants[:, :, NM * GC:ZW].rearrange("p j (m c) -> p j m c", c=C)
                    else:
                        o = quadrants[:, :, 0:NM * GC].rearrange("p j (m g c) -> p g j m c", m=NM, c=C)[:, place]
                    yield (o, src[:, g * H:(g + 1) * H].rearrange("p (j m c) -> p j m c", m=NM, c=C),
                           scale * (2.0 if g == G - 1 else 1.0))

            for name, raw, dst, ready, whole in (("wx", wx_raw, wx, wx_ready, 1.0), ("wh", wh_raw, wh, wh_ready, 0.5)):
                dve.wait_ge(w_loaded[name], 16 * NM)
                for kc in range(NM):
                    for o, i, scale in reorder(dst[:, kc, :], raw[:, kc, :], whole):
                        dve.tensor_scalar(o, i, scale, None, ALU.mult).then_inc(ready, 1)
                if name == "wx":
                    dve.wait_ge(w_loaded["b"], 16)
                    for o, i, scale in reorder(b_all[:, :], b_raw[:, :], 1.0):
                        dve.tensor_scalar(o, i, scale, None, ALU.mult).then_inc(b_ready, 1)
                    dve.wait_ge(b_ready, G)
                    for q in range(XQ):
                        evacuate_projection(Blk(0, 0), q)
            dve.wait_ge(w_loaded["cq"], 16 * NQ)
            dve.tensor_scalar(cond_2[:, :], cond_q[:, :], 2.0, None, ALU.mult).then_inc(cond_doubled, 1)
            dve.wait_ge(cond_doubled, 1)
            for m in both:
                dve.transpose(h_first[:, m, :], cond_2[:, m * C:(m + 1) * C]).then_inc(ht_ready[m], 1)
            for q in range(XQ):
                evacuate_projection(Blk(0, 1), q)
            dve.wait_ge(consts_made, 2)
            dve.reduce_sum(own_row[:, :], ident[:, :].rearrange("p (r b) -> p b r", b=B), AX.X).then_inc(zeroed, 1)

            dve.wait_ge(w_loaded["cond"], 48)
            dve.reduce_sum(c_stat[:, 0:1], c_in[:, :], AX.X).then_inc(ln_step, 1)
            dve.wait_ge(ln_step, 1)
            dve.tensor_scalar(c_stat[:, 1:2], c_stat[:, 0:1], -1.0 / D, None, ALU.mult).then_inc(ln_step, 1)
            dve.wait_ge(ln_step, 2)
            dve.tensor_scalar(c_mid[:, :], c_in[:, :], c_stat[:, 1:2], None, ALU.add).then_inc(ln_step, 1)
            dve.wait_ge(ln_step, 3)
            dve.tensor_tensor(c_sq[:, :], c_mid[:, :], c_mid[:, :], ALU.mult).then_inc(ln_step, 1)
            dve.wait_ge(ln_step, 4)
            dve.reduce_sum(c_stat[:, 2:3], c_sq[:, :], AX.X).then_inc(ln_step, 1)
            dve.wait_ge(ln_step, 5)
            dve.tensor_scalar(c_stat[:, 3:4], c_stat[:, 2:3], 1.0 / D, LN_EPS, ALU.mult, ALU.add).then_inc(ln_step, 1)

            def cell_products(s, m, n):
                now = gates[s % 2][m]
                dve.wait_ge(gates_ready[m], n)
                dve.scalar_tensor_tensor(prod[m][:, :], now[:, 0:2 * C], 1.0, now[:, 2 * C:4 * C],
                                         ALU.add, ALU.mult).then_inc(prod_ready[m], 1)

            def new_cell(s, m, n):
                dve.wait_ge(prod_ready[m], n)
                dve.scalar_tensor_tensor(gates[(s + 1) % 2][m][:, GC:GC + C], prod[m][:, C:2 * C], 0.5,
                                         prod[m][:, 0:C], ALU.mult, ALU.add).then_inc(cell_ready[m], 1)

            def new_hidden(s, m, n):
                dve.wait_ge(tanc_ready[m], n)
                dve.scalar_tensor_tensor(hid[m][:, :], gate_o[:, C * m:C * (m + 1)], 1.0, tanc[m][:, :],
                                         ALU.add, ALU.mult).then_inc(hid_ready[m], 1)

            def transpose_hidden(k, s, m, n):
                dve.wait_ge(hid_ready[m], n)
                dve.transpose(h_t[k.par][:, m, s, :], hid[m][:, :]).then_inc(ht_ready[m], 1)

            def make_weights(k, s):
                if k == 0 and s == 0:
                    dve.wait_ge(ln_pow, 1)
                    dve.scalar_tensor_tensor(c_sq[:, :], c_mid[:, :], c_stat[:, 4:5], c_gamma[:, :],
                                             ALU.mult, ALU.mult).then_inc(ln_pow, 1)
                    dve.wait_ge(ln_pow, 2)
                    dve.tensor_tensor(c_norm[:, :], c_sq[:, :], c_beta[:, :], ALU.add).then_inc(ln_step, 1)
                if k == 0 and s == 1:
                    dve.wait_ge(cond_t_psum, 1)
                    dve.tensor_copy(c_t[:, :, :], aux[:, 0:2 * B].rearrange("p (k b) -> p k b", k=2))\
                       .then_inc(cond_t_ready, 1)
                if k == 1 and s == 0:
                    dve.wait_ge(w_loaded["down"], 16 * NM)
                    dve.tensor_scalar(down[:, :, :], down_raw[:, :, :], 0.5, None, ALU.mult).then_inc(down_ready, 1)

            def one_block(k, front):
                a, e, f = follower(k), early(k), k.plus(2)
                for s in range(TB):
                    n = k.k * TB + (s + 1)
                    cell_products(s, 0, n)
                    new_cell(s, 0, n)
                    cell_products(s, 1, n)
                    new_cell(s, 1, n)
                    new_hidden(s, 0, n)
                    if s == 0 and k.at_least(2):
                        dve.wait_ge(xp_ready, k.k * 2 - 2)
                    transpose_hidden(k, s, 0, n)
                    new_hidden(s, 1, n)
                    transpose_hidden(k, s, 1, n)
                    if s == 0 and e:
                        mask_u(e)
                    if s == 1 and a:
                        mask_u(a)
                    if s in (2, 3) and front:
                        evacuate_projection(f, s - 2)
                    if s == 3 and e:
                        mask_v(e)
                    if s in (5, 7) and front:
                        evacuate_projection(f, 2 + s // 7)
                    if s == 5 and e:
                        add_residual(e)
                    if s == 5 and a:
                        mask_v(a)
                    if s == 7 and a:
                        add_residual(a)
                    if not k.at_least(EARLY + 1):
                        make_weights(k.k, s)

            schedule(dve, one_block)
            for part in (mask_u, mask_v, add_residual):
                for a in last_jobs:
                    part(a)

        @block.gpsimd
        def _(pool):
            pool.memset(ident[:, :], 0.0).then_inc(consts_made, 1)
            pool.wait_ge(consts_made, 1)
            pool.affine_select(out=ident[:, :], in_=ident[:, :], compare_op=ALU.not_equal, fill=1.0, base=0,
                               pattern=[[-1, P]], channel_multiplier=1).then_inc(consts_made, 1)
            pool.memset(neg_half[:, :], -0.5).then_inc(consts_made, 1)
            pool.memset(one_win[:, :], 0.0).then_inc(consts_made, 1)
            pool.wait_ge(consts_made, 4)
            pool.memset(one_win[:, B:2 * B], 1.0).then_inc(consts_made, 1)
            pool.dma_start(b2_row[:, :, :], bias2.rearrange("(a q n) -> a q n", a=1, q=4)).then_inc(w_loaded["b2row"], 16)
            pool.dma_start(c_in[:, :], cond).then_inc(w_loaded["cond"], 16)
            pool.dma_start(c_gamma[:, :], gamma.partition_broadcast(B)).then_inc(w_loaded["cond"], 16)
            pool.dma_start(c_beta[:, :], beta.partition_broadcast(B)).then_inc(w_loaded["cond"], 16)

            def permute_x(f):
                pool.wait_ge(x_loaded[f.par], (f.turn + 1) * 16)
                if f.at_least(2):
                    pool.wait_ge(xt_psum, f.k - 1)
                natural = perm(x_nat[f.par][:, :])
                pool.tensor_tensor(x_perm[f.par][:, :].rearrange("p (m j c) -> p m j c", m=NM, j=NQ),
                                   natural, natural, ALU.add).then_inc(x_permuted, 1)

            def keep_x(f):
                pool.wait_ge(xt_ready, f.k + 1)
                if f.at_least(2):
                    pool.wait_ge(xp_ready, f.k * 2 - 2)
                pool.tensor_tensor(x_keep[f.par][:, :, :], x_t[f.par][:, :, :], x_t[f.par][:, :, :], ALU.add)\
                    .then_inc(x_kept, 1)

            def add_h(k):
                pool.wait_ge(x_kept, k.k + 1)
                dst = xp[k.par] if k.at_least(EARLY) else xp_early[k.k]
                if k.at_least(EARLY + 2):
                    pool.wait_ge(y_ready[0], k.k - EARLY - 1)
                for m in both:
                    pool.wait_ge(ht_ready[m], k.k * TB + (TB + 1))
                    tokens = "p (b t) -> p b t"
                    pool.tensor_tensor(dst[:, m, :].rearrange(tokens, b=B),
                                       x_keep[k.par][:, m, :].rearrange(tokens, b=B),
                                       h_t[k.par][:, m, :, 0:B].rearrange("p t b -> p b t"), ALU.add)\
                        .then_inc(xp_ready, 1)

            for par in range(3):
                permute_x(Blk(0, 0, par))
            for par in range(2):
                keep_x(Blk(0, par))
            pool.wait_ge(ln_step, 6)
            pool.tensor_tensor(c_stat[:, 4:5], c_stat[:, 3:4], neg_half[:, :], ALU.pow).then_inc(ln_pow, 1)

            def one_block(k, front):
                if k.plus(3).exists():
                    permute_x(k.plus(3))
                add_h(k)
                if front:
                    keep_x(k.plus(2))

            schedule(pool, one_block, 2)


_INS = ["x", "cond_1024", "L0_cond_Wx", "L0_cond_Wh", "L0_cond_b", "L1_cond_base_up", "L1_cond_base_down",
        "L1_cond_ln_gamma", "L1_cond_ln_beta", "L1_cond_W1", "L1_cond_bias1", "L1_cond_W2", "L1_cond_bias2"]


def kernel(**inputs):
    import numpy as _np
    import concourse.bacc as _bacc
    from concourse import mybir as _mybir
    from concourse.bass_utils import run_bass_kernel_spmd as _run

    nc = _bacc.Bacc("TRN2", target_bir_lowering=False, num_devices=1)
    arrays, args = {}, []
    for name in _INS:
        a = _np.ascontiguousarray(inputs[name])
        arrays[f"in_{name}"] = a
        args.append(nc.dram_tensor(f"in_{name}", a.shape, _mybir.dt.from_np(a.dtype), kind="ExternalInput").ap())
    args.append(nc.dram_tensor("out_0", (B, T, D), F32, kind="ExternalOutput").ap())
    lstm_adapter(nc, *args)
    r = _run(nc, [arrays], core_ids=[0])
    return r.results[0]["out_0"]
```

```python
from contextlib import ExitStack

import concourse.bass as bass
from concourse import mybir

F32 = mybir.dt.float32
ALU = mybir.AluOpType
ACT = mybir.ActivationFunctionType
AX = mybir.AxisListType

B, T, D, H = 16, 256, 256, 256
G = 4
P = 128
NQ, NM, C = 4, 2, 32
TB = 8
NBLK = T // TB
RANK = 8
GC = 3 * C
OC = NM * C
ZW = NM * GC + OC
OG = NM
Z_EARLY = 52
XQ = NQ
XW = G * H // XQ
LN_EPS = 1e-5
QUARTERS = (1, 2, 0, 3)
W_STEPS = 6
EARLY = 3
N_PIECES = 16
PIECES = ((0, 0, 0, 4, 4, 7, 10, 14, 16), (0, 2, 4, 6, 8, 10, 12, 14, 16), (0, 2, 6, 7, 8, 10, 11, 12, 16))
WARM_UP = 4
PEELED = 3


def lstm_adapter(nc, x, cond, Wx, Wh, b, base_up, base_down, gamma, beta, W1, bias1, W2, bias2, out):
    ctx = ExitStack()
    with ctx:
        def sb(name, shape):
            return ctx.enter_context(nc.sbuf_tensor(name, shape, F32))

        def psum(name):
            return ctx.enter_context(nc.psum_tensor(name, [P, 512], F32))

        def sem(name):
            return ctx.enter_context(nc.semaphore(name))

        ident = sb("ident", [P, P])
        zeros = sb("zeros", [P, P])
        ones = sb("ones", [P, P])
        gelu_0 = sb("gelu_0", [1, 1])
        one_win = sb("one_win", [1, 3 * B])
        own_row = sb("own_row", [P, B])
        neg_half = sb("neg_half", [B, 1])
        wx_raw = sb("wx_raw", [P, NM, G * H])
        wh_raw = sb("wh_raw", [P, NM, G * H])
        b_raw = sb("b_raw", [P, G * H])
        wx = sb("wx", [P, NM, G * H])
        wh = sb("wh", [P, NM, G * H])
        b_all = sb("b_all", [P, G * H])
        down_raw = sb("down_raw", [P, NM, D])
        down = sb("down", [P, NM, D])
        up_raw = sb("up_raw", [P, NM, D])
        up_t = sb("up_t", [P, 2, D])
        a1_t = sb("a1_t", [P, D])
        b2_t = sb("b2_t", [P, D])
        b1_w = sb("b1_w", [P, 2, P])
        a2_w = sb("a2_w", [P, NM, P])
        c_in = sb("c_in", [B, D])
        c_gamma = sb("c_gamma", [B, D])
        c_beta = sb("c_beta", [B, D])
        c_mid = sb("c_mid", [B, D])
        c_sq = sb("c_sq", [B, D])
        c_norm = sb("c_norm", [B, D])
        c_stat = sb("c_stat", [B, 5])
        c_t = sb("c_t", [P, 2, B])
        w1 = sb("w1", [P, 2, D])
        b1_col = sb("b1_col", [P, 2])
        hid_win = sb("hid_win", [P, 2, 3 * B])
        w2_tiles = [sb(f"w2_{n}", [P, 2, D * RANK]) for n in range(3)]
        w2 = {q: w2_tiles[n % 3] for n, q in enumerate(QUARTERS)}
        b2_row = sb("b2_row", [1, 4, D * RANK])
        w_tmp = sb("w_tmp", [P, 2, D])
        x_nat = [sb(f"x_nat{i}", [P, D]) for i in range(2)]
        x_perm = [sb(f"x_perm{i}", [P, D]) for i in range(2)]
        x_t = [sb(f"x_t{i}", [P, NM, P]) for i in range(2)]
        x_keep = [sb(f"x_keep{i}", [P, NM, P]) for i in range(2)]
        proj = [sb(f"proj{i}", [P, G * H]) for i in range(2)]
        seed = [sb(f"seed{i}", [P, TB, ZW]) for i in range(2)]
        cond_q = sb("cond_q", [P, NM * C])
        cond_2 = sb("cond_2", [P, NM * C])
        h_first = sb("h_first", [P, NM, 32])
        gates = [[sb(f"gates{i}_{m}", [P, GC + C]) for m in range(NM)] for i in range(2)]
        gate_o = sb("gate_o", [P, OC])
        prod = [sb(f"prod{m}", [P, 2 * C]) for m in range(NM)]
        tanc = [sb(f"tanc{m}", [P, C]) for m in range(NM)]
        hid = [sb(f"hid{m}", [P, C]) for m in range(NM)]
        h_t = [sb(f"h_t{i}", [P, NM, TB, 32]) for i in range(2)]
        xp = [sb(f"xp{i}", [P, NM, P]) for i in range(2)]
        xp_early = [sb(f"xp_early{i}", [P, NM, P]) for i in range(EARLY)]
        lanes = range(2)
        u_own = [sb(f"u_own{i}", [P, P]) for i in lanes]
        v_own = [sb(f"v_own{i}", [P, P]) for i in lanes]
        act_t = [sb(f"act_t{i}", [P, 2, P]) for i in lanes]
        y_t = [sb(f"y_t{i}", [P, NM, P]) for i in lanes]
        y_nat = [[sb(f"y_nat{lane}_{i}", [P, D]) for i in range(2)] for lane in lanes]

        z_bank = [psum(f"z{m}") for m in range(NM)]
        o_bank = psum("z_o")
        aux = psum("aux")
        out_bank = psum("out_bank")
        x_bank = [psum(f"x_bank{i}") for i in range(2)]
        mid_bank, up_bank = (aux, x_bank[0]), (out_bank, x_bank[1])

        consts_made = sem("consts_made")
        zeroed = sem("zeroed")
        w_loaded = {n: sem(f"{n}_loaded") for n in
                    ("wx", "wh", "b", "down", "up", "cond", "cq", "w1", "b2row")}
        w2_loaded = [sem(f"w2_loaded{q}") for q in range(4)]
        wx_ready, wh_ready = sem("wx_ready"), sem("wh_ready")
        b_psum = sem("b_psum")
        b_ready, down_ready = sem("b_ready"), sem("down_ready")
        bits_set = sem("bits_set")
        cond_doubled = sem("cond_doubled")
        ln_step, ln_pow = sem("ln_step"), sem("ln_pow")
        cond_t_psum, cond_t_ready = sem("cond_t_psum"), sem("cond_t_ready")
        hidden_psum, hidden_ready = sem("hidden_psum"), sem("hidden_ready")
        up_psum, up_ready = sem("up_psum"), sem("up_ready")
        w_psum, w_copied = sem("w_psum"), sem("w_copied")
        wt_psum, wt_ready = sem("wt_psum"), sem("wt_ready")
        x_loaded = [sem(f"x_loaded{i}") for i in range(2)]
        x_permuted = sem("x_permuted")
        xt_psum, xt_ready = sem("xt_psum"), sem("xt_ready")
        x_kept = sem("x_kept")
        xz_psum, xz_ready = sem("xz_psum"), sem("xz_ready")
        seed_loaded = [sem(f"seed_loaded{i}") for i in range(2)]
        both = range(NM)
        seeded = [sem(f"seeded{m}") for m in both]
        seeded_o, zo_ready, gate_o_ready = sem("seeded_o"), sem("zo_ready"), sem("gate_o_ready")
        z_ready = [sem(f"z_ready{m}") for m in both]
        gates_ready = [sem(f"gates_ready{m}") for m in both]
        prod_ready = [sem(f"prod_ready{m}") for m in both]
        cell_ready = [sem(f"cell_ready{m}") for m in both]
        tanc_ready = [sem(f"tanc_ready{m}") for m in both]
        hid_ready = [sem(f"hid_ready{m}") for m in both]
        ht_ready = [sem(f"ht_ready{m}") for m in both]
        xp_ready = sem("xp_ready")
        u_psum, u_ready = ([sem(f"{n}{i}") for i in lanes] for n in ("u_psum", "u_ready"))
        mid_psum, act_ready = ([sem(f"{n}{i}") for i in lanes] for n in ("mid_psum", "act_ready"))
        v_psum, v_ready = ([sem(f"{n}{i}") for i in lanes] for n in ("v_psum", "v_ready"))
        out_psum, y_ready = ([sem(f"{n}{i}") for i in lanes] for n in ("out_psum", "y_ready"))
        yt_psum, y_copied = ([sem(f"{n}{i}") for i in lanes] for n in ("yt_psum", "y_copied"))
        stored = [[sem(f"stored{lane}_{i}") for i in range(2)] for lane in lanes]

        block = ctx.enter_context(nc.Block())

        def perm(ap):
            return ap.rearrange("p (j m c) -> p m j c", j=NQ, m=NM)

        def reorder(dst, src, scale):
            quadrants = dst.rearrange("p (j n) -> p j n", n=ZW)
            for g in range(G):
                place = {0: 0, 1: 1, 3: 2}.get(g)
                if place is None:
                    o = quadrants[:, :, NM * GC:ZW].rearrange("p j (m c) -> p j m c", c=C)
                else:
                    o = quadrants[:, :, 0:NM * GC].rearrange("p j (m g c) -> p g j m c", m=NM, c=C)[:, place]
                yield (o, src(g).rearrange("p (j m c) -> p j m c", m=NM, c=C),
                       scale * (2.0 if g == G - 1 else 1.0))

        class Blk:

            def __init__(self, it, par, shift=0):
                self.k = it * 2 + (par + shift)
                self.par = (par + shift) % 2
                self.turn = it + (par + shift) // 2
                self.it, self.p, self.s = it, par, shift

            def plus(self, n):
                return Blk(self.it, self.p, self.s + n)

            def at_least(self, n):
                return not isinstance(self.k, int) or self.k >= n

            def exists(self):
                return not isinstance(self.k, int) or 0 <= self.k < NBLK

        def schedule(eng, one_block, last=1):
            for pair in range(PEELED):
                for par in range(2):
                    one_block(Blk(pair, par), True)
            with eng.Fori(PEELED, NBLK // 2 - last) as it:
                for par in range(2):
                    one_block(Blk(it, par), True)
            for pair in range(NBLK // 2 - last, NBLK // 2):
                for par in range(2):
                    one_block(Blk(pair, par), pair < NBLK // 2 - 1)

        class Job:

            def __init__(self, blk, lane):
                self.blk, self.lane = blk, lane
                self.seq = blk.plus(-EARLY) if lane == 0 else blk
                self.xp = xp[blk.par] if lane == 0 else xp_early[blk.k]

        def follower(k):
            return Job(k.plus(-1), 0) if k.at_least(EARLY + 1) else None

        def early(k):
            n = k.k - (NBLK - 2) if isinstance(k.k, int) else -1
            return Job(Blk(0, 0, n), 1) if 0 <= n < EARLY else None

        end = Blk(NBLK // 2, 0)
        last, last_early = follower(end), early(end)

        @block.sync
        def _(sp):
            def load_x(f):
                first = f.k * TB if isinstance(f.k, int) else sp.snap(f.k * TB)
                if f.at_least(2):
                    sp.wait_ge(x_permuted, f.k - 1)
                sp.dma_start(x_nat[f.par][:, :], x[:, bass.ds(first, TB), :]).then_inc(x_loaded[f.par], 16)

            def load_seed(f):
                consumed = f.k * TB - TB if isinstance(f.k, int) else sp.snap(f.k * TB - TB)
                if f.at_least(2):
                    for gone in (*seeded, seeded_o):
                        sp.wait_ge(gone, consumed)
                    sp.wait_ge(xz_ready, f.k * XQ + XQ)
                for j in range(NQ):
                    if not f.at_least(2):
                        sp.wait_ge(xz_ready, f.k * XQ + (j + 1))
                    sp.dma_start(seed[f.par][32 * j:32 * j + B, :, :], proj[f.par][:, ZW * j:ZW * (j + 1)])\
                      .then_inc(seed_loaded[f.par], 16)

            def store_y(a):
                first = a.blk.k * TB if isinstance(a.blk.k, int) else sp.snap(a.blk.k * TB)
                sp.wait_ge(y_copied[a.lane], a.seq.k + 1)
                sp.dma_start(out[:, bass.ds(first, TB), :], y_nat[a.lane][a.seq.par][:, :])\
                  .then_inc(stored[a.lane][a.seq.par], 16)

            by_half = "(j m c) n -> m j c n"

            def load_halves(dst, src, name):
                for m in both:
                    sp.dma_start(dst[:, m, :], src.rearrange(by_half, j=NQ, m=NM)[m]).then_inc(w_loaded[name], 16)

            w2_q = W2.rearrange("(k p) (q n) -> q p k n", p=P, q=4)

            def load_w2(q):
                sp.dma_start(w2[q][:, :, :], w2_q[q]).then_inc(w2_loaded[q], 16)

            load_x(Blk(0, 0))
            sp.wait_ge(zeroed, 1)
            sp.dma_start(b_raw[0:1, :], b.rearrange("(a n) -> a n", a=1)).then_inc(w_loaded["b"], 16)
            load_halves(wx_raw, Wx, "wx")
            load_x(Blk(0, 1))
            sp.dma_start(c_in[:, :], cond).then_inc(w_loaded["cond"], 16)
            sp.dma_start(c_gamma[:, :], gamma.partition_broadcast(B)).then_inc(w_loaded["cond"], 16)
            sp.dma_start(c_beta[:, :], beta.partition_broadcast(B)).then_inc(w_loaded["cond"], 16)
            load_halves(wh_raw, Wh, "wh")
            load_seed(Blk(0, 0))
            load_x(Blk(0, 0, 2))
            sp.dma_start(w1[:, :, :], W1.rearrange("(k p) n -> p k n", p=P)).then_inc(w_loaded["w1"], 16)
            sp.dma_start(b1_col[:, :], bias1.rearrange("(k p) -> p k", p=P),
                         allow_slow_non_contiguous=True).then_inc(w_loaded["w1"], 16)
            load_halves(up_raw, base_up, "up")
            load_w2(QUARTERS[0])
            load_seed(Blk(0, 1))
            load_halves(down_raw, base_down, "down")

            def one_block(k, front):
                if k.plus(3).exists():
                    load_x(k.plus(3))
                if not k.at_least(1):
                    load_w2(QUARTERS[1])
                if front:
                    load_seed(k.plus(2))
                if not k.at_least(1):
                    load_w2(QUARTERS[2])
                if not k.at_least(2) and k.k == 1:
                    sp.wait_ge(w_psum, 1)
                    load_w2(QUARTERS[3])
                done = follower(k.plus(-1))
                if done and done.seq.exists():
                    store_y(done)
                if early(k):
                    store_y(early(k))

            schedule(sp, one_block, 2)
            store_y(follower(Blk(NBLK // 2 - 1, 1)))
            store_y(last_early)
            store_y(last)
            for lane, jobs in enumerate((NBLK - EARLY, EARLY)):
                for i in range(2):
                    sp.wait_ge(stored[lane][i], 16 * ((jobs + 1 - i) // 2))

        @block.scalar
        def _(act):
            act.wait_ge(zeroed, 2)
            act.activation(gelu_0[:, :], zeros[0:1, 0:1], ACT.Gelu)

            def evacuate_x(f):
                act.wait_ge(xt_psum, f.k + 1)
                if f.at_least(2):
                    act.wait_ge(xz_psum, (f.k - 1) * XQ)
                    act.wait_ge(x_kept, f.k - 1)
                act.activation(x_t[f.par][:, :, :],
                               aux[:, 0:NM * P].rearrange("p (m t) -> p m t", m=NM), ACT.Copy,
                               scale=0.5).then_inc(xt_ready, 1)

            def seed_bank(buf, s, m):
                act.activation(z_bank[m][:, 0:GC], seed[buf][:, s, GC * m:GC * (m + 1)], ACT.Copy)\
                   .then_inc(seeded[m], 1)

            def seed_o(buf, s):
                act.activation(o_bank[:, 0:OC], seed[buf][:, s, NM * GC:ZW], ACT.Copy).then_inc(seeded_o, 1)

            def gelu_mid(a):
                act.wait_ge(mid_psum[a.lane], a.seq.k + 1)
                if a.seq.at_least(1):
                    act.wait_ge(out_psum[a.lane], a.seq.k)
                act.activation(act_t[a.lane][:, :, :],
                               mid_bank[a.lane][:, 0:2 * P].rearrange("p (l t) -> p l t", l=2),
                               ACT.Gelu).then_inc(act_ready[a.lane], 1)

            def copy_y(a):
                act.wait_ge(yt_psum[a.lane], a.seq.k + 1)
                if a.seq.at_least(2):
                    act.wait_ge(stored[a.lane][a.seq.par], a.seq.turn * 16)
                act.activation(perm(y_nat[a.lane][a.seq.par][:, :]),
                               up_bank[a.lane][:, 0:D].rearrange("p (m j c) -> p m j c", m=NM, j=NQ),
                               ACT.Copy).then_inc(y_copied[a.lane], 1)

            def make_weights(k, s):
                if k == 0 and s == 3:
                    act.wait_ge(w_loaded["w1"], 32)
                    act.wait_ge(hidden_psum, 1)
                    for i in range(2):
                        act.activation(hid_win[:, i, B:2 * B], aux[:, i * B:(i + 1) * B], ACT.Gelu,
                                       bias=b1_col[:, i:i + 1]).then_inc(hidden_ready, 1)
                if k == 0 and s in (4, 5):
                    act.wait_ge(up_psum, s - 3)
                    act.activation(up_t[:, s - 4, :], out_bank[:, 0:D], ACT.Copy).then_inc(up_ready, 1)
                if k >= 1 and ((k - 1) * TB + s) % W_STEPS == W_STEPS - 1:
                    n = ((k - 1) * TB + s) // W_STEPS
                    q = QUARTERS[n]
                    act.wait_ge(w_psum, n + 1)
                    src = out_bank[:, 0:D]
                    if q == 0:
                        ins = act.activation(a1_t[:, :].rearrange("p (m j c) -> p m j c", m=NM, j=NQ), perm(src),
                                             ACT.Copy)
                    elif q == 1:
                        ins = act.activation(w_tmp[:, 0, :], src, ACT.Copy)
                    elif q == 2:
                        ins = act.activation(w_tmp[:, 1, :].rearrange("p (m j c) -> p m j c", m=NM, j=NQ), perm(src),
                                             ACT.Copy, scale=0.5)
                    else:
                        ins = act.activation(b2_t[:, :], src, ACT.Copy)
                    ins.then_inc(w_copied, 1)
                if k == 2 and s in (2, 6):
                    n = s // 4
                    act.wait_ge(wt_psum, n + 1)
                    act.activation((b1_w, a2_w)[n][:, :, :], aux[:, 0:2 * P].rearrange("p (l t) -> p l t", l=2),
                                   ACT.Copy).then_inc(wt_ready, 1)

            evacuate_x(Blk(0, 0))
            act.wait_ge(zeroed, 3)
            for j in range(NQ):
                act.dma_start(cond_q[32 * j:32 * j + B, :], cond[:, NM * C * j:NM * C * (j + 1)])\
                   .then_inc(w_loaded["cq"], 16)

            def reorder_all(dst, raw, name, scale_all, ready):
                act.wait_ge(w_loaded[name], 16 * NM)
                for kc in both:
                    for o, i, scale in reorder(dst[:, kc, :], lambda g: raw[:, kc, g * H:(g + 1) * H], scale_all):
                        act.activation(o, i, ACT.Copy, scale=scale).then_inc(ready, 1)

            reorder_all(wx, wx_raw, "wx", 1.0, wx_ready)
            evacuate_x(Blk(0, 1))
            reorder_all(wh, wh_raw, "wh", 0.5, wh_ready)
            act.wait_ge(bits_set, 1)
            act.wait_ge(seed_loaded[0], 16 * NQ)
            for m in both:
                seed_bank(0, 0, m)
            seed_o(0, 0)

            def one_block(k, front):
                a, e, done = follower(k), early(k), follower(k.plus(-1))
                for s in range(TB):
                    n = k.k * TB + (s + 1)
                    more = s < TB - 1 or front or k.p == 0
                    ahead, s_next = (k, s + 1) if s < TB - 1 else (k.plus(1), 0)

                    def gates_of(m):
                        act.wait_ge(z_ready[m], n)
                        act.activation(gates[s % 2][m][:, 0:GC], z_bank[m][:, 0:GC], ACT.Tanh,
                                       scale=0.5).then_inc(gates_ready[m], 1)

                    def tanh_o(m):
                        cols = slice(C * m, C * (m + 1))
                        return act.activation(gate_o[:, cols], o_bank[:, cols], ACT.Tanh, scale=0.5)

                    def tanh_cell(m):
                        act.wait_ge(cell_ready[m], n)
                        act.activation(tanc[m][:, :], gates[(s + 1) % 2][m][:, GC:GC + C], ACT.Tanh,
                                       scale=0.5).then_inc(tanc_ready[m], 1)

                    gates_of(0)
                    gates_of(1)
                    act.wait_ge(zo_ready, n)
                    tanh_o(0)
                    tanh_cell(0)
                    tanh_o(1).then_inc(gate_o_ready, 1)
                    if more:
                        act.wait_ge(gates_ready[0], n)
                        seed_bank(ahead.par, s_next, 0)
                    tanh_cell(1)
                    if more:
                        act.wait_ge(gates_ready[1], n)
                        seed_bank(ahead.par, s_next, 1)
                        act.wait_ge(gate_o_ready, n)
                        seed_o(ahead.par, s_next)
                    if s == TB - 2 and (front or k.p == 0):
                        ahead = k.plus(1)
                        act.wait_ge(seed_loaded[ahead.par], (ahead.turn + 1) * (16 * NQ))
                    if s == 0 and not k.at_least(1):
                        evacuate_x(k.plus(2))
                    if not k.at_least(EARLY + 1):
                        make_weights(k.k, s)
                    if s == 2 and e:
                        gelu_mid(e)
                    if s == 3 and a:
                        gelu_mid(a)
                    if s == 0 and done and done.seq.exists():
                        copy_y(done)
                    if s == 7 and e:
                        copy_y(e)
                    if s == (6 if a else 7) and k.plus(3).exists():
                        evacuate_x(k.plus(3))

            schedule(act, one_block, 2)
            copy_y(follower(Blk(NBLK // 2 - 1, 1)))
            gelu_mid(last_early)
            gelu_mid(last)
            copy_y(last_early)
            copy_y(last)

        @block.tensor
        def _(pe):
            def transpose_x(f, halves):
                if 0 in halves:
                    pe.wait_ge(x_permuted, f.k + 1)
                for m in halves:
                    ins = pe.transpose(aux[:, m * P:(m + 1) * P], x_perm[f.par][:, m * P:(m + 1) * P], ident[:, :])
                if 1 in halves:
                    ins.then_inc(xt_psum, 1)

            def project(f, pieces):
                for i in pieces:
                    q, half, kc = i // 4, i // 2 % 2, i % 2
                    if i == 0:
                        pe.wait_ge(xt_ready, f.k + 1)
                    if i == 4 and not f.at_least(1):
                        pe.wait_ge(b_ready, G)
                    if i % 4 == 0 and (f.at_least(1) or q >= 2):
                        pe.wait_ge(xz_ready, f.k * XQ + (q - 1))
                    cols = slice(half * XW // 2, (half + 1) * XW // 2)
                    dst, rhs = x_bank[q % 2][:, cols], wx[:, kc, q * XW:(q + 1) * XW][:, cols]
                    if not f.at_least(2):
                        dst = dst.rearrange("p (g n) -> p g n", g=G // 2)
                        rhs = wx_raw[:, kc, :].rearrange("p (g j n) -> p j g n", g=G, j=NQ)\
                            [:, q, half * G // 2:(half + 1) * G // 2]
                    ins = pe.matmul(dst, x_t[f.par][:, kc, :], rhs, start=(kc == 0), stop=(kc == 1))
                    if i % 4 == 3:
                        ins.then_inc(xz_psum, 1)

            def down_rank(a):
                if a.lane == 0 and a.seq.at_least(1):
                    pe.wait_ge(v_ready[0], a.seq.k)
                pe.wait_ge(wt_ready, 2)
                pe.wait_ge(xp_ready, a.blk.k * 2 + 2)
                for m in both:
                    ins = pe.matmul(mid_bank[a.lane][:, 0:P], a2_w[:, m, :], a.xp[:, m, :],
                                    start=(m == 0), stop=(m == 1))
                ins.then_inc(u_psum[a.lane], 1)

            def down_full(a, parts):
                for i in parts:
                    l, part = divmod(i, 3)
                    if i == 0:
                        pe.wait_ge(w_copied, 4)
                        pe.wait_ge(down_ready, 1)
                        pe.wait_ge(u_ready[a.lane], a.seq.k + 1)
                    cols = slice(l * P, (l + 1) * P)
                    lhs, rhs = ((down[:, part, cols], a.xp[:, part, :]) if part < 2 else
                                (b2_t[:, cols], u_own[a.lane][:, :]))
                    ins = pe.matmul(mid_bank[a.lane][:, cols], lhs, rhs, start=(part == 0), stop=(part == 2))
                    if i == 5:
                        ins.then_inc(mid_psum[a.lane], 1)

            def up_rank(a):
                pe.wait_ge(act_ready[a.lane], a.seq.k + 1)
                for l in range(2):
                    ins = pe.matmul(mid_bank[a.lane][:, 0:P], b1_w[:, l, :], act_t[a.lane][:, l, :],
                                    start=(l == 0), stop=(l == 1))
                ins.then_inc(v_psum[a.lane], 1)

            def up_full(a, parts):
                for i in parts:
                    m, part = divmod(i, 3)
                    if i == 0:
                        if a.seq.at_least(1):
                            pe.wait_ge(y_copied[a.lane], a.seq.k)
                        pe.wait_ge(up_ready, 2)
                        pe.wait_ge(v_ready[a.lane], a.seq.k + 1)
                    cols = slice(m * P, (m + 1) * P)
                    lhs, rhs = ((up_t[:, part, cols], act_t[a.lane][:, part, :]) if part < 2 else
                                (a1_t[:, cols], v_own[a.lane][:, :]))
                    ins = pe.matmul(up_bank[a.lane][:, cols], lhs, rhs, start=(part == 0), stop=(part == 2))
                    if i == 5:
                        ins.then_inc(out_psum[a.lane], 1)

            def transpose_y(a, halves):
                if 0 in halves:
                    pe.wait_ge(y_ready[a.lane], a.seq.k + 1)
                for m in halves:
                    ins = pe.transpose(up_bank[a.lane][:, m * P:(m + 1) * P], y_t[a.lane][:, m, :], ident[:, :])
                if 1 in halves:
                    ins.then_inc(yt_psum[a.lane], 1)

            def make_weights(k, s):
                if k == 0 and s == 2:
                    pe.wait_ge(ln_step, 7)
                    pe.wait_ge(xt_ready, 3)
                    for i in range(2):
                        ins = pe.transpose(aux[:, i * B:(i + 1) * B], c_norm[:, i * P:(i + 1) * P], ident[0:B, 0:B])
                    ins.then_inc(cond_t_psum, 1)
                if k == 0 and s == 3:
                    pe.wait_ge(w_loaded["w1"], 32)
                    pe.wait_ge(cond_t_ready, 1)
                    for i in range(2):
                        for kc in range(2):
                            ins = pe.matmul(aux[:, i * B:(i + 1) * B], w1[:, kc, i * P:(i + 1) * P], c_t[:, kc, :],
                                            start=(kc == 0), stop=(kc == 1))
                    ins.then_inc(hidden_psum, 1)
                if k == 0 and s in (4, 5):
                    if s == 4:
                        pe.wait_ge(w_loaded["up"], 32)
                    else:
                        pe.wait_ge(up_ready, 1)
                    for m in both:
                        ins = pe.transpose(out_bank[:, m * P:(m + 1) * P], up_raw[:, m, (s - 4) * P:(s - 3) * P],
                                           ident[:, :])
                    ins.then_inc(up_psum, 1)
                if k >= 1:
                    n, i = divmod((k - 1) * TB + s, W_STEPS)
                    q, odd, part = QUARTERS[n], i // 3, i % 3
                    if n == 0 and i == 0:
                        pe.wait_ge(w_loaded["b2row"], 16)
                        pe.wait_ge(hidden_ready, 2)
                        pe.wait_ge(up_ready, 2)
                    elif i == 0:
                        pe.wait_ge(w_copied, n)
                    if i == 1:
                        pe.wait_ge(w2_loaded[q], 16)
                    window = slice((1 - odd) * B, (3 - odd) * B)
                    for j in range(NQ):
                        r = 2 * j + odd
                        if part == 0:
                            lhs, rhs = one_win[:, window], b2_row[:, q, :].rearrange("p (d r) -> p r d", r=RANK)[:, r, :]
                        else:
                            lhs = hid_win[:, part - 1, window]
                            rhs = w2[q][:, part - 1, :].rearrange("p (d r) -> p r d", r=RANK)[:, r, :]
                        ins = pe.matmul(out_bank[32 * j:32 * (j + 1), 0:D], lhs, rhs, start=(i == 0),
                                        stop=(i == W_STEPS - 1))
                    if i == W_STEPS - 1:
                        ins.then_inc(w_psum, 1)
                if k == 2 and s in (2, 6):
                    n = s // 4
                    pe.wait_ge(w_copied, n + 1)
                    if n == 0:
                        pe.wait_ge(xt_ready, k + 3)
                    else:
                        pe.wait_ge(wt_ready, 1)
                    for i in range(2):
                        ins = pe.transpose(aux[:, i * P:(i + 1) * P], w_tmp[:, n, i * P:(i + 1) * P], ident[:, :])
                    ins.then_inc(wt_psum, 1)

            pe.wait_ge(zeroed, 2)
            for i in range(WARM_UP):
                ins = pe.matmul((*z_bank, o_bank)[i % 3][:, 0:GC], zeros[:, :], zeros[:, 0:GC], start=True, stop=True)
            ins.then_inc(bits_set, 1)
            pe.wait_ge(consts_made, 6)

            transpose_x(Blk(0, 0), both)
            pe.wait_ge(w_loaded["b"], 16)
            for i, bank in enumerate((out_bank, x_bank[1])):
                pe.matmul(bank[:, :], ones[:, :], b_raw[:, i * 2 * H:(i + 1) * 2 * H],
                          start=True, stop=True).then_inc(b_psum, 1)
            pe.wait_ge(w_loaded["wx"], 16 * NM)
            project(Blk(0, 0), range(N_PIECES))
            transpose_x(Blk(0, 1), both)
            project(Blk(0, 1), range(N_PIECES // 2))

            pe.wait_ge(wh_ready, 2 * G)

            def one_block(k, front):
                a, e, done, f = follower(k), early(k), follower(k.plus(-1)), k.plus(2)
                x_steps = (5, 6) if a else (7, 7)
                pieces = PIECES[2 if a else 1 if k.at_least(1) else 0]
                for s in range(TB):
                    n = k.k * TB + (s + 1)
                    if s > 0:
                        h_prev = h_t[k.par][:, :, s - 1, 0:B]
                    elif k.at_least(1):
                        h_prev = h_t[1 - k.par][:, :, TB - 1, 0:B]
                    else:
                        h_prev = h_first[:, :, 0:B]
                    z, o = (0, GC), (0, OC)
                    order = ((0, 0, z), (0, 1, (0, Z_EARLY)), (1, 0, z), (0, 1, (Z_EARLY, GC)), (1, 1, z),
                             (0, OG, o), (1, OG, o))
                    for i, (kc, m, (lo, hi)) in enumerate(order):
                        if kc not in [other[0] for other in order[:i]]:
                            pe.wait_ge(ht_ready[kc], n)
                        if kc == 0 and lo == 0:
                            pe.wait_ge(seeded_o if m == OG else seeded[m], n)
                        for j in range(NQ):
                            col = j * ZW + m * GC
                            ins = pe.matmul((*z_bank, o_bank)[m][32 * j:32 * j + B, lo:hi], h_prev[:, kc, :],
                                            wh[:, kc, col + lo:col + hi], start=False, stop=(kc == 1),
                                            skip_group_check=True)
                        if kc == 1:
                            ins.then_inc(zo_ready if m == OG else z_ready[m], 1)
                    if s == 0 and done and done.seq.exists():
                        transpose_y(done, (1,))
                    if s == 7 and not front and k.p == 1:
                        pe.wait_ge(v_ready[1], last_early.seq.k)
                        down_rank(last_early)
                    if s in x_steps and k.plus(3).exists():
                        if not k.at_least(1):
                            pe.wait_ge(hidden_ready, 2)
                        if k.at_least(EARLY - 1) and not k.at_least(EARLY):
                            pe.wait_ge(wt_ready, 2)
                        if a and s == x_steps[0]:
                            pe.wait_ge(v_ready[0], a.seq.k + 1)
                        transpose_x(k.plus(3), [m for m in both if x_steps[m] == s])
                    if a:
                        if s == 0:
                            if front:
                                pe.wait_ge(xt_ready, f.k + 1)
                            down_rank(a)
                        if s in (2, 3):
                            down_full(a, range(3 * s - 6, 3 * s - 3))
                        if s == 4:
                            up_rank(a)
                        if s in (5, 6):
                            up_full(a, range(3 * s - 15, 3 * s - 12))
                        if s == 7:
                            transpose_y(a, (0,))
                    if e:
                        if s == 0:
                            pe.wait_ge(xz_ready, NBLK * XQ)
                            down_rank(e)
                        if s in (1, 2):
                            down_full(e, range(0, 5) if s == 1 else range(5, 6))
                        if s == 3:
                            up_rank(e)
                        if s in (4, 5, 6):
                            up_full(e, range(2 * s - 8, 2 * s - 6))
                        if s == 7:
                            transpose_y(e, both)
                    if front:
                        if not k.at_least(1):
                            if s == 0:
                                transpose_x(f, both)
                            if s < 2:
                                project(Blk(0, 1), range(8 + 4 * s, 12 + 4 * s))
                            if s == 2:
                                pe.wait_ge(wx_ready, 2 * G)
                        project(f, range(pieces[s], pieces[s + 1]))
                    if not k.at_least(EARLY + 1):
                        make_weights(k.k, s)

            schedule(pe, one_block, 2)
            transpose_y(follower(Blk(NBLK // 2 - 1, 1)), (1,))
            down_full(last_early, range(0, 4))
            down_rank(last)
            down_full(last_early, range(4, 6))
            down_full(last, range(0, 3))
            up_rank(last_early)
            down_full(last, range(3, 6))
            up_full(last_early, range(0, 3))
            up_rank(last)
            up_full(last_early, range(3, 6))
            up_full(last, range(6))
            transpose_y(last_early, both)
            transpose_y(last, both)

        @block.vector
        def _(dve):
            def evacuate_projection(f, q):
                dve.wait_ge(xz_psum, f.k * XQ + (q + 1))
                if q == 0 and f.at_least(2):
                    dve.wait_ge(seed_loaded[f.par], f.turn * (16 * NQ))
                dve.tensor_tensor(proj[f.par][:, q * XW:(q + 1) * XW], x_bank[q % 2][:, 0:XW],
                                  b_all[:, q * XW:(q + 1) * XW], ALU.add).then_inc(xz_ready, 1)

            def mask(bank, dst, done):
                dve.tensor_tensor(dst[:, :].rearrange("p (b t) -> p b t", b=B),
                                  bank[:, 0:P].rearrange("p (b t) -> p b t", b=B),
                                  own_row[:, :].unsqueeze(2).to_broadcast([P, B, TB]), ALU.mult).then_inc(done, 1)

            def mask_u(a):
                dve.wait_ge(u_psum[a.lane], a.seq.k + 1)
                mask(mid_bank[a.lane], u_own[a.lane], u_ready[a.lane])

            def mask_v(a):
                dve.wait_ge(v_psum[a.lane], a.seq.k + 1)
                mask(mid_bank[a.lane], v_own[a.lane], v_ready[a.lane])

            def add_residual(a):
                dve.wait_ge(out_psum[a.lane], a.seq.k + 1)
                dve.tensor_tensor(y_t[a.lane][:, :, :], a.xp[:, :, :],
                                  up_bank[a.lane][:, 0:NM * P].rearrange("p (m t) -> p m t", m=NM), ALU.add)\
                   .then_inc(y_ready[a.lane], 1)

            dve.memset(b_raw[:, :], 0.0).then_inc(zeroed, 1)
            dve.memset(zeros[:, :], 0.0).then_inc(zeroed, 1)
            dve.memset(cond_q[:, :], 0.0).then_inc(zeroed, 1)
            dve.memset(hid_win[:, :, :], 0.0).then_inc(zeroed, 1)
            for m in both:
                dve.memset(gates[0][m][:, GC:GC + C], 0.0).then_inc(zeroed, 1)
            for i in range(2):
                dve.memset(seed[i][:, :, :], 0.0).then_inc(zeroed, 1)

            def evacuate_first(f, q):
                dve.wait_ge(xz_psum, f.k * XQ + (q + 1))
                src = x_bank[q % 2][:, 0:XW].rearrange("p (g m c) -> p g m c", g=G, m=NM)
                dst, bias = (t[:, q * XW:(q + 1) * XW] for t in (proj[f.par], b_all))
                for gate, place, scale in ((0, 0, 1.0), (1, 1, 1.0), (2, None, 1.0), (3, 2, 2.0)):
                    def part(t):
                        if place is None:
                            return t[:, NM * GC:ZW].rearrange("p (m c) -> p m c", m=NM)
                        return t[:, 0:NM * GC].rearrange("p (m g c) -> p g m c", m=NM, c=C)[:, place]
                    ins = dve.scalar_tensor_tensor(part(dst), src[:, gate], scale, part(bias), ALU.mult, ALU.add)
                ins.then_inc(xz_ready, 1)

            def b_bank(g):
                return (out_bank, x_bank[1])[g // 2][:, g % 2 * H:(g % 2 + 1) * H]

            for g, (o, i, scale) in enumerate(reorder(b_all[:, :], b_bank, 1.0)):
                dve.wait_ge(b_psum, g // 2 + 1)
                dve.tensor_scalar(o, i, scale, None, ALU.mult).then_inc(b_ready, 1)
            dve.wait_ge(b_ready, G)
            for q in range(XQ):
                evacuate_first(Blk(0, 0), q)
            dve.wait_ge(w_loaded["cq"], 16 * NQ)
            dve.tensor_scalar(cond_2[:, :], cond_q[:, :], 2.0, None, ALU.mult).then_inc(cond_doubled, 1)
            dve.wait_ge(cond_doubled, 1)
            for m in both:
                dve.transpose(h_first[:, m, :], cond_2[:, m * C:(m + 1) * C]).then_inc(ht_ready[m], 1)

            dve.wait_ge(w_loaded["cond"], 48)
            dve.reduce_sum(c_stat[:, 0:1], c_in[:, :], AX.X).then_inc(ln_step, 1)
            dve.wait_ge(ln_step, 1)
            dve.tensor_scalar(c_stat[:, 1:2], c_stat[:, 0:1], -1.0 / D, None, ALU.mult).then_inc(ln_step, 1)
            dve.wait_ge(ln_step, 2)
            dve.tensor_scalar(c_mid[:, :], c_in[:, :], c_stat[:, 1:2], None, ALU.add).then_inc(ln_step, 1)
            dve.wait_ge(ln_step, 3)
            dve.tensor_tensor(c_sq[:, :], c_mid[:, :], c_mid[:, :], ALU.mult).then_inc(ln_step, 1)
            dve.wait_ge(ln_step, 4)
            dve.reduce_sum(c_stat[:, 2:3], c_sq[:, :], AX.X).then_inc(ln_step, 1)
            dve.wait_ge(ln_step, 5)
            dve.tensor_scalar(c_stat[:, 3:4], c_stat[:, 2:3], 1.0 / D, LN_EPS, ALU.mult, ALU.add).then_inc(ln_step, 1)

            for q in range(2):
                evacuate_first(Blk(0, 1), q)
            dve.wait_ge(consts_made, 2)
            dve.reduce_sum(own_row[:, :], ident[:, :].rearrange("p (r b) -> p b r", b=B), AX.X).then_inc(zeroed, 1)

            def cell_products(s, m, n):
                now = gates[s % 2][m]
                dve.wait_ge(gates_ready[m], n)
                dve.scalar_tensor_tensor(prod[m][:, :], now[:, 0:2 * C], 1.0, now[:, 2 * C:4 * C],
                                         ALU.add, ALU.mult).then_inc(prod_ready[m], 1)

            def new_cell(s, m, n):
                dve.wait_ge(prod_ready[m], n)
                dve.scalar_tensor_tensor(gates[(s + 1) % 2][m][:, GC:GC + C], prod[m][:, C:2 * C], 0.5,
                                         prod[m][:, 0:C], ALU.mult, ALU.add).then_inc(cell_ready[m], 1)

            def new_hidden(s, m, n):
                dve.wait_ge(tanc_ready[m], n)
                dve.scalar_tensor_tensor(hid[m][:, :], gate_o[:, C * m:C * (m + 1)], 1.0, tanc[m][:, :],
                                         ALU.add, ALU.mult).then_inc(hid_ready[m], 1)

            def transpose_hidden(k, s, m, n):
                dve.wait_ge(hid_ready[m], n)
                dve.transpose(h_t[k.par][:, m, s, :], hid[m][:, :]).then_inc(ht_ready[m], 1)

            def make_weights(k, s):
                if k == 0 and s == 0:
                    dve.wait_ge(ln_pow, 1)
                    dve.scalar_tensor_tensor(c_sq[:, :], c_mid[:, :], c_stat[:, 4:5], c_gamma[:, :],
                                             ALU.mult, ALU.mult).then_inc(ln_pow, 1)
                if k == 0 and s == 1:
                    dve.wait_ge(ln_pow, 2)
                    dve.tensor_tensor(c_norm[:, :], c_sq[:, :], c_beta[:, :], ALU.add).then_inc(ln_step, 1)
                if k == 0 and s == 2:
                    dve.wait_ge(cond_t_psum, 1)
                    dve.tensor_copy(c_t[:, :, :], aux[:, 0:2 * B].rearrange("p (k b) -> p k b", k=2))\
                       .then_inc(cond_t_ready, 1)
                if k == 1 and s == 0:
                    dve.wait_ge(w_loaded["down"], 16 * NM)
                    dve.tensor_scalar(down[:, :, :], down_raw[:, :, :], 0.5, None, ALU.mult).then_inc(down_ready, 1)

            def one_block(k, front):
                a, e, f = follower(k), early(k), k.plus(2)
                for s in range(TB):
                    n = k.k * TB + (s + 1)
                    if s == 0 and k.at_least(2):
                        dve.wait_ge(xp_ready, k.k * 2 - 2)
                    cell_products(s, 0, n)
                    new_cell(s, 0, n)
                    cell_products(s, 1, n)
                    new_cell(s, 1, n)
                    new_hidden(s, 0, n)
                    transpose_hidden(k, s, 0, n)
                    if s == 7 and not front and k.p == 1:
                        mask_u(last_early)
                    new_hidden(s, 1, n)
                    transpose_hidden(k, s, 1, n)
                    if s == 0 and a:
                        mask_u(a)
                    if s == 0 and e:
                        mask_u(e)
                    if s == 3 and e:
                        mask_v(e)
                    if s == 4 and a:
                        mask_v(a)
                    if s == 6 and a:
                        add_residual(a)
                    if s == 6 and e:
                        add_residual(e)
                    if not k.at_least(1) and s < 2:
                        evacuate_first(Blk(0, 1), 2 + s)
                    if front and k.at_least(1) and s in (1, 3, 6, 7):
                        evacuate_projection(f, (1, 3, 6, 7).index(s))
                    if not k.at_least(1) and s in (2, 5, 6, 7):
                        evacuate_projection(f, max(0, s - 4))
                    if not k.at_least(EARLY + 1):
                        make_weights(k.k, s)

            schedule(dve, one_block)
            mask_u(last)
            mask_v(last_early)
            mask_v(last)
            add_residual(last_early)
            add_residual(last)

        @block.gpsimd
        def _(pool):
            pool.memset(ident[:, :], 0.0).then_inc(consts_made, 1)
            pool.wait_ge(consts_made, 1)
            pool.affine_select(out=ident[:, :], in_=ident[:, :], compare_op=ALU.not_equal, fill=1.0, base=0,
                               pattern=[[-1, P]], channel_multiplier=1).then_inc(consts_made, 1)
            pool.memset(neg_half[:, :], -0.5).then_inc(consts_made, 1)
            pool.memset(one_win[:, :], 0.0).then_inc(consts_made, 1)
            pool.wait_ge(consts_made, 4)
            pool.memset(one_win[:, B:2 * B], 1.0).then_inc(consts_made, 1)
            pool.memset(ones[:, :], 1.0).then_inc(consts_made, 1)

            def permute_x(f):
                pool.wait_ge(x_loaded[f.par], (f.turn + 1) * 16)
                if f.at_least(2):
                    pool.wait_ge(xt_psum, f.k - 1)
                natural = perm(x_nat[f.par][:, :])
                pool.tensor_tensor(x_perm[f.par][:, :].rearrange("p (m j c) -> p m j c", m=NM, j=NQ),
                                   natural, natural, ALU.add).then_inc(x_permuted, 1)

            def keep_x(f):
                pool.wait_ge(xt_ready, f.k + 1)
                if f.at_least(2):
                    pool.wait_ge(xp_ready, f.k * 2 - 2)
                pool.tensor_tensor(x_keep[f.par][:, :, :], x_t[f.par][:, :, :], x_t[f.par][:, :, :], ALU.add)\
                    .then_inc(x_kept, 1)

            def add_h(k):
                pool.wait_ge(x_kept, k.k + 1)
                dst = xp[k.par] if k.at_least(EARLY) else xp_early[k.k]
                if k.at_least(EARLY + 2):
                    pool.wait_ge(y_ready[0], k.k - EARLY - 1)
                for m in both:
                    pool.wait_ge(ht_ready[m], k.k * TB + (TB + 1))
                    tokens = "p (b t) -> p b t"
                    pool.tensor_tensor(dst[:, m, :].rearrange(tokens, b=B),
                                       x_keep[k.par][:, m, :].rearrange(tokens, b=B),
                                       h_t[k.par][:, m, :, 0:B].rearrange("p t b -> p b t"), ALU.add)\
                        .then_inc(xp_ready, 1)

            permute_x(Blk(0, 0))
            pool.dma_start(b2_row[:, :, :], bias2.rearrange("(a q n) -> a q n", a=1, q=4)).then_inc(w_loaded["b2row"], 16)
            for par in (1, 2):
                permute_x(Blk(0, 0, par))
            for par in range(2):
                keep_x(Blk(0, par))
            pool.wait_ge(ln_step, 6)
            pool.tensor_tensor(c_stat[:, 4:5], c_stat[:, 3:4], neg_half[:, :], ALU.pow).then_inc(ln_pow, 1)

            def one_block(k, front):
                if k.plus(3).exists():
                    permute_x(k.plus(3))
                add_h(k)
                if front:
                    keep_x(k.plus(2))

            schedule(pool, one_block, 2)


_INS = ["x", "cond_1024", "L0_cond_Wx", "L0_cond_Wh", "L0_cond_b", "L1_cond_base_up", "L1_cond_base_down",
        "L1_cond_ln_gamma", "L1_cond_ln_beta", "L1_cond_W1", "L1_cond_bias1", "L1_cond_W2", "L1_cond_bias2"]


def kernel(**inputs):
    import numpy as _np
    import concourse.bacc as _bacc
    from concourse import mybir as _mybir
    from concourse.bass_utils import run_bass_kernel_spmd as _run

    nc = _bacc.Bacc("TRN2", target_bir_lowering=False, num_devices=1)
    arrays, args = {}, []
    for name in _INS:
        a = _np.ascontiguousarray(inputs[name])
        arrays[f"in_{name}"] = a
        args.append(nc.dram_tensor(f"in_{name}", a.shape, _mybir.dt.from_np(a.dtype), kind="ExternalInput").ap())
    args.append(nc.dram_tensor("out_0", (B, T, D), F32, kind="ExternalOutput").ap())
    lstm_adapter(nc, *args)
    r = _run(nc, [arrays], core_ids=[0])
    return r.results[0]["out_0"]
```
